# Optimizing a Trainium2 kernel written in Bass

```python
import numpy as np
import jax
import jax.numpy as jnp

def _softmax(x, axis=-1):
    return jax.nn.softmax(x, axis=axis)

def _gelu(x):
    return jax.nn.gelu(x, approximate=True)

def _silu(x):
    return jax.nn.silu(x)

def _sigmoid(x):
    return jax.nn.sigmoid(x)

def _layernorm(x, axis=-1, eps=1e-05):
    m = jnp.mean(x, axis=axis, keepdims=True)
    v = jnp.var(x, axis=axis, keepdims=True)
    return (x - m) / jnp.sqrt(v + eps)

def _scatter_add(tgt, idx, src, axis=0):
    return tgt.at[idx].add(src)

def _segment_sum(src, seg, n):
    return jax.ops.segment_sum(src, seg, n)
kernel_name = 'mk_cond_resid_d4_seqx_r4_5e9815'

def setup_inputs(seed: int=0):
    np.random.seed(seed)
    _w = jnp.asarray

    def _rec_inputs():
        import jax
        import jax.numpy as jnp
        _rk = jax.random.key(seed)
        x = -0.000125 + 0.9999 * jax.random.normal(jax.random.fold_in(_rk, 1), (64, 64, 256), jnp.float32)
        _lenS = 64 - jax.random.randint(jax.random.fold_in(_rk, 7), (64,), 0, max(1, 64 // 4) + 1, jnp.int32)
        _lenS2 = 64 - jax.random.randint(jax.random.fold_in(_rk, 8), (64,), 0, max(1, 64 // 4) + 1, jnp.int32)
        cond_1024 = -0.00493535 + 1.00056 * jax.random.normal(jax.random.fold_in(_rk, 11), (64, 256), jnp.float32)
        return (x, cond_1024)
    x, cond_1024 = _rec_inputs()

    def _L0_cond_setup():
        import jax, jax.numpy as jnp
        import numpy as np
        N, T, D, H = (64, 128, 256, 256)
        key = jax.random.key(seed)
        k1, k2, k3, k4 = jax.random.split(key, 4)
        x = jax.random.normal(k1, (N, T, D), dtype=jnp.float32)
        h0 = jax.random.normal(k2, (N, H), dtype=jnp.float32)
        Wx = jax.random.normal(k3, (D, H), dtype=jnp.float32) / np.sqrt(D)
        Wh = jax.random.normal(k4, (H, H), dtype=jnp.float32) / np.sqrt(H)
        b = jnp.zeros((H,), dtype=jnp.float32)
        return {'x': x, 'h0': h0, 'Wx': Wx, 'Wh': Wh, 'b': b}
    _L0_cond_all = _L0_cond_setup()
    _L0_cond_in = {k: v for k, v in _L0_cond_all.items() if k in ('Wx', 'Wh', 'b')}
    del _L0_cond_all

    def _L1_cond_setup():
        import jax, jax.numpy as jnp
        import numpy as np
        NHID = 256
        NHEAD = 16
        HEAD_DIM = 64
        B, L = (8, 1024)
        key = jax.random.key(seed)
        ks = jax.random.split(key, 12)
        s_in = 1.0 / np.sqrt(NHID)
        s_o = 1.0 / np.sqrt(NHEAD * HEAD_DIM)
        return {'x': jax.random.normal(ks[0], (B, L, NHID), dtype=jnp.float32), 'ax': jax.random.normal(ks[1], (B, NHID), dtype=jnp.float32), 'WQ_w': jax.random.normal(ks[2], (NHID, NHEAD * HEAD_DIM), dtype=jnp.float32) * s_in, 'WQ_b': jnp.zeros((NHEAD * HEAD_DIM,), dtype=jnp.float32), 'WK_w': jax.random.normal(ks[3], (NHID, NHEAD * HEAD_DIM), dtype=jnp.float32) * s_in, 'WK_b': jnp.zeros((NHEAD * HEAD_DIM,), dtype=jnp.float32), 'WV_w': jax.random.normal(ks[4], (NHID, NHEAD * HEAD_DIM), dtype=jnp.float32) * s_in, 'WV_b': jnp.zeros((NHEAD * HEAD_DIM,), dtype=jnp.float32), 'WO_w': jax.random.normal(ks[5], (NHEAD * HEAD_DIM, NHID), dtype=jnp.float32) * s_o, 'WO_b': jnp.zeros((NHID,), dtype=jnp.float32)}
    _L1_cond_all = _L1_cond_setup()
    _L1_cond_in = {k: v for k, v in _L1_cond_all.items() if k in ('WQ_w', 'WQ_b', 'WK_w', 'WK_b', 'WV_w', 'WV_b', 'WO_w', 'WO_b')}
    del _L1_cond_all

    def _L2_cond_setup():
        import jax, jax.numpy as jnp
        import numpy as np
        import math
        D = 256
        H = 256
        key = jax.random.key(seed)
        k1, k2, k3, k4 = jax.random.split(key, 4)
        x = jax.random.normal(k1, (64, 128, D), dtype=jnp.float32)
        h0 = jax.random.normal(k2, (64, H), dtype=jnp.float32)
        Wx = jax.random.normal(k3, (D, 4 * H), dtype=jnp.float32) / math.sqrt(D)
        Wh = jax.random.normal(k4, (H, 4 * H), dtype=jnp.float32) / math.sqrt(H)
        b = jnp.zeros((4 * H,), dtype=jnp.float32)
        return {'x': x, 'h0': h0, 'Wx': Wx, 'Wh': Wh, 'b': b}
    _L2_cond_all = _L2_cond_setup()
    _L2_cond_in = {k: v for k, v in _L2_cond_all.items() if k in ('Wx', 'Wh', 'b')}
    del _L2_cond_all

    def _L3_cond_setup():
        import jax, jax.numpy as jnp
        import numpy as np
        import math
        D = 256
        H = 256
        N = 128
        T = 128
        key = jax.random.key(seed)
        k1, k2, k3, k4 = jax.random.split(key, 4)
        x = jax.random.normal(k1, (N, T, D), dtype=jnp.float32)
        h0 = jax.random.normal(k2, (N, H), dtype=jnp.float32)
        Wx = jax.random.normal(k3, (D, H), dtype=jnp.float32) / math.sqrt(D)
        Wh = jax.random.normal(k4, (H, H), dtype=jnp.float32) / math.sqrt(H)
        b = jnp.zeros((H,), dtype=jnp.float32)
        return {'x': x, 'h0': h0, 'Wx': Wx, 'Wh': Wh, 'b': b}
    _L3_cond_all = _L3_cond_setup()
    _L3_cond_in = {k: v for k, v in _L3_cond_all.items() if k in ('Wx', 'Wh', 'b')}
    del _L3_cond_all
    return {'x': x, 'cond_1024': cond_1024, 'L0_cond_Wx': _L0_cond_in['Wx'], 'L0_cond_Wh': _L0_cond_in['Wh'], 'L0_cond_b': _L0_cond_in['b'], 'L1_cond_WQ_w': _L1_cond_in['WQ_w'], 'L1_cond_WQ_b': _L1_cond_in['WQ_b'], 'L1_cond_WK_w': _L1_cond_in['WK_w'], 'L1_cond_WK_b': _L1_cond_in['WK_b'], 'L1_cond_WV_w': _L1_cond_in['WV_w'], 'L1_cond_WV_b': _L1_cond_in['WV_b'], 'L1_cond_WO_w': _L1_cond_in['WO_w'], 'L1_cond_WO_b': _L1_cond_in['WO_b'], 'L2_cond_Wx': _L2_cond_in['Wx'], 'L2_cond_Wh': _L2_cond_in['Wh'], 'L2_cond_b': _L2_cond_in['b'], 'L3_cond_Wx': _L3_cond_in['Wx'], 'L3_cond_Wh': _L3_cond_in['Wh'], 'L3_cond_b': _L3_cond_in['b']}

def reference(x, cond_1024, L0_cond_Wx, L0_cond_Wh, L0_cond_b, L1_cond_WQ_w, L1_cond_WQ_b, L1_cond_WK_w, L1_cond_WK_b, L1_cond_WV_w, L1_cond_WV_b, L1_cond_WO_w, L1_cond_WO_b, L2_cond_Wx, L2_cond_Wh, L2_cond_b, L3_cond_Wx, L3_cond_Wh, L3_cond_b):
    import jax
    import jax.numpy as jnp

    def _L0_cond_ref(x, h0, Wx, Wh, b):
        import jax, jax.numpy as jnp
        import numpy as np
        N, T, D, H = (64, 128, 256, 256)
        xW = jnp.einsum('ntd,dh->nth', x, Wx) + b
        xW_t = jnp.swapaxes(xW, 0, 1)

        def step(prev_h, xw):
            next_h = jnp.tanh(prev_h @ Wh + xw)
            return (next_h, next_h)
        _, h_t = jax.lax.scan(step, h0, xW_t)
        return jnp.swapaxes(h_t, 0, 1)

    def _L1_cond_ref(x, ax, WQ_w, WQ_b, WK_w, WK_b, WV_w, WV_b, WO_w, WO_b):
        import jax, jax.numpy as jnp
        import numpy as np
        NHID = 256
        NHEAD = 16
        HEAD_DIM = 64
        B, L = (8, 1024)
        Bx, Lx, H = x.shape
        nh, d = (NHEAD, HEAD_DIM)
        q = (x @ WQ_w + WQ_b).reshape(Bx, Lx, nh, d)
        k = (x @ WK_w + WK_b).reshape(Bx, Lx, nh, d)
        ak = (ax @ WK_w + WK_b).reshape(Bx, 1, nh, d)
        av = (ax @ WV_w + WV_b).reshape(Bx, 1, nh, d)
        pad_k = jnp.pad(k, ((0, 0), (1, 1), (0, 0), (0, 0)))
        k_shift = jnp.stack([pad_k[:, t:Lx + t] for t in range(3)], axis=3)
        akb = jnp.broadcast_to(ak, (Bx, Lx, nh, d))[:, :, :, None, :]
        avb = jnp.broadcast_to(av, (Bx, Lx, nh, d))[:, :, :, None, :]
        K = jnp.concatenate([akb, k_shift], axis=3)
        V = jnp.concatenate([avb, k_shift], axis=3)
        scores = jnp.einsum('blhd,blhjd->blhj', q, K) / jnp.sqrt(jnp.float32(d))
        alphas = jax.nn.softmax(scores, axis=-1)
        att = jnp.einsum('blhj,blhjd->blhd', alphas, V).reshape(Bx, Lx, nh * d)
        return att @ WO_w + WO_b

    def _L2_cond_ref(x, h0, Wx, Wh, b):
        import jax, jax.numpy as jnp
        import numpy as np
        import math
        D = 256
        H = 256
        Hdim = h0.shape[1]
        xW = jnp.einsum('ntd,dk->ntk', x, Wx) + b
        c0 = jnp.zeros_like(h0)

        def step(carry, xw_t):
            prev_h, prev_c = carry
            a = xw_t + prev_h @ Wh
            i = jax.nn.sigmoid(a[:, :Hdim])
            f = jax.nn.sigmoid(a[:, Hdim:2 * Hdim])
            o = jax.nn.sigmoid(a[:, 2 * Hdim:3 * Hdim])
            g = jnp.tanh(a[:, 3 * Hdim:])
            next_c = f * prev_c + i * g
            next_h = o * jnp.tanh(next_c)
            return ((next_h, next_c), next_h)
        xW_t = jnp.swapaxes(xW, 0, 1)
        _, hs = jax.lax.scan(step, (h0, c0), xW_t)
        hn = jnp.swapaxes(hs, 0, 1)
        return hn

    def _L3_cond_ref(x, h0, Wx, Wh, b):
        import jax, jax.numpy as jnp
        import numpy as np
        import math
        D = 256
        H = 256
        N = 128
        T = 128
        xW = jnp.einsum('ntd,dh->nth', x, Wx) + b

        def step(prev_h, xw_t):
            next_h = jnp.tanh(prev_h @ Wh + xw_t)
            return (next_h, next_h)
        _, h_t = jax.lax.scan(step, h0, jnp.swapaxes(xW, 0, 1))
        return jnp.swapaxes(h_t, 0, 1)
    x = x + _L0_cond_ref(x, cond_1024, L0_cond_Wx, L0_cond_Wh, L0_cond_b)
    x = x + _L1_cond_ref(x, cond_1024, L1_cond_WQ_w, L1_cond_WQ_b, L1_cond_WK_w, L1_cond_WK_b, L1_cond_WV_w, L1_cond_WV_b, L1_cond_WO_w, L1_cond_WO_b)
    x = x + _L2_cond_ref(x, cond_1024, L2_cond_Wx, L2_cond_Wh, L2_cond_b)
    x = x + _L3_cond_ref(x, cond_1024, L3_cond_Wx, L3_cond_Wh, L3_cond_b)
    return x

_drawn_inputs = setup_inputs


def setup_inputs(seed=0):
    import zlib

    import numpy as np

    out = dict(_drawn_inputs(seed))
    spreads = {'L0_cond_b': (0.0, 0.1),
     'L1_cond_WQ_b': (0.0, 0.1),
     'L1_cond_WK_b': (0.0, 0.1),
     'L1_cond_WV_b': (0.0, 0.353),
     'L1_cond_WO_b': (0.0, 0.1),
     'L2_cond_b': (0.0, 0.364),
     'L3_cond_b': (0.0, 0.1)}
    factors = {}
    for name, (base, spread) in spreads.items():
        noise = np.random.default_rng([zlib.crc32(name.encode()), seed]).standard_normal(out[name].shape)
        drawn = base * np.exp(spread * noise) if base else spread * noise
        out[name] = jnp.asarray(drawn.astype(out[name].dtype))
    for name, factor in factors.items():
        out[name] = (out[name] * factor).astype(out[name].dtype)
    return out
```

```python
from contextlib import ExitStack

import concourse.bass as bass
from concourse import mybir

N, T, D = 64, 64, 256
HEADS, HEAD_DIM = 16, 64
E = HEADS * HEAD_DIM
P = 128
KT = D // P
F = E // P
PER_TILE = HEAD_DIM // F
STEPS = 4
C = STEPS * N
CHUNKS = T // STEPS
SLOTS = 8
J = 4
WIN = (STEPS + 2) * N
KRING, XRING = 4, 3

RNN0 = 1
SPLIT = 8
KEYS = 9
PAD = 17
SCORES = 18
HEADSUM = 26
SHIFT = 27
EXP = 28
NORM = 29
MIX = 30
ATTSPLIT = 31
OUTPROJ = 32
X2 = 40
LSTM = 42
HIDDEN = 43
RNN3 = 51
LAST = RNN3 + 2 * (STEPS - 1)
DEPTH = LAST // SLOTS
SM = 7
ADDS = F - 1

B_RNN0, B_LSTM, B_RNN3, B_Q, B_K, B_V, B_O, B_END = 0, 2, 10, 12, 20, 28, 36, 38


def sequence_stack_kernel(nc, x_in, cond_in, bias_in, ones_in, rnn0_in, rnn3_in, lstm_x_in, lstm_h_in,
                          wq_in, wk_in, wv_in, wo_in, out):
    f32, f32r = mybir.dt.float32, mybir.dt.float32r
    ALU, ACT = mybir.AluOpType, mybir.ActivationFunctionType

    ctx = ExitStack()
    with ctx:
        def sb(name, shape, dt=f32):
            return ctx.enter_context(nc.sbuf_tensor(name, [P, *shape], dt))

        def bank(name, banks=1):
            return ctx.enter_context(nc.psum_tensor(name, [P, banks * 512], f32))

        def sem(name):
            return ctx.enter_context(nc.semaphore(name))

        X = sb("X", [KT, T * N])
        rnn_w = [sb("rnn0_w", [2, KT, D]), sb("rnn3_w", [2, KT, D])]
        lstm_wx = sb("lstm_wx", [KT, 4 * D])
        lstm_wh = sb("lstm_wh", [KT, 4 * D])
        wq = [sb("wq_hi", [KT, F, P], f32r), sb("wq_lo", [KT, F, P], f32r)]
        wk = [sb("wk_hi", [KT, F, P], f32r), sb("wk_lo", [KT, F, P], f32r)]
        wo = [sb("wo_hi", [F, D], f32r), sb("wo_lo", [F, D], f32r)]
        bias = sb("bias", [B_END])
        half_bias = sb("half_bias", [6])
        ones = sb("head_ones", [P])
        keys = sb("keys", [KRING, F, WIN])
        relay_k = sb("relay_k", [F, N])
        relay_v = sb("relay_v", [F, N])
        x1_hi = sb("x1_hi", [XRING, KT, C], f32r)
        x1_lo = sb("x1_lo", [XRING, KT, C], f32r)
        prod = sb("prod", [2, J, C])
        score = sb("score", [J, C])
        W = sb("W", [J, C])
        pair = sb("pair", [2, C])
        single = sb("single", [C])
        alpha = sb("alpha", [J, C])
        mix = sb("mix", [J, C])
        att = sb("att", [2, C])
        att_hi = sb("att_hi", [2, C], f32r)
        att_lo = sb("att_lo", [2, C], f32r)
        h = [sb("h0", [2, KT, N]), sb("h3", [2, KT, N])]
        h2 = sb("h2", [2, KT, N])
        gates = sb("gates", [F, N])
        cell = sb("cell", [KT, N])

        room = keys[:, 2:4].rearrange("p a f w -> p (a f w)")
        stage_k = room[:, 0:KT * E].rearrange("p (k f m) -> p k f m", k=KT, f=F)
        stage_v = room[:, KT * E:2 * KT * E].rearrange("p (k f m) -> p k f m", k=KT, f=F)
        stage_q = room[:, 2 * KT * E:3 * KT * E].rearrange("p (k f m) -> p k f m", k=KT, f=F)
        stage_o = prod[:].rearrange("p a j c -> p (a j c)").rearrange("p (f m) -> p f m", f=F)

        ps_rnn = [bank("ps_rnn0"), bank("ps_rnn3")]
        ps_lstm = bank("ps_lstm")
        ps_q = bank("ps_q")
        ps_k = bank("ps_k")
        ps_s = bank("ps_s", 2)
        ps_o = bank("ps_o")

        ld_first = sem("ld_first")
        ld_x = [sem(f"ld_x{i}") for i in range(4)]
        ld_k, ld_v, ld_q, ld_o = sem("ld_k"), sem("ld_v"), sem("ld_q"), sem("ld_o")
        ld_ones, ld_lstm, ld_rnn3 = sem("ld_ones"), sem("ld_lstm"), sem("ld_rnn3")
        ld_relay = sem("ld_relay")
        X_LOADS = [(0, 1), (1, 2), (2, 6), (6, CHUNKS)]
        w_hi = sem("w_hi")
        w_lo = sem("w_lo")
        relay_mm = sem("relay_mm")
        relay_done = sem("relay_done")
        padded = sem("padded")
        half_done = sem("half_done")
        rnn_mm = [sem("rnn0_mm"), sem("rnn3_mm")]
        lstm_mm = sem("lstm_mm")
        k_mm, q_mm, o_mm = sem("k_mm"), sem("q_mm"), sem("o_mm")
        s_mm = sem("s_mm")
        rnn_h = [sem("rnn0_h"), sem("rnn3_h")]
        gates_done, tanh_c = sem("gates_done"), sem("tanh_c")
        k_done = sem("k_done")
        s_copied, exp_done = sem("s_copied"), sem("exp_done")
        x1_hi_done, att_hi_done = sem("x1_hi_done"), sem("att_hi_done")
        x1_done, x3_done, x4_done = sem("x1_done"), sem("x3_done"), sem("x4_done")
        x1_lo_done, x2_done = sem("x1_lo_done"), sem("x2_done")
        prod_done, mix_done, att_lo_done = sem("prod_done"), sem("mix_done"), sem("att_lo_done")
        softmax = sem("softmax")
        cell_chain = sem("cell_chain")
        h2_done = sem("h2_done")
        score_add = sem("score_add")
        mix_pair = sem("mix_pair")
        att_done = sem("att_done")
        stored = sem("stored")

        def wait(eng, semaphore, value):
            if not isinstance(value, int) or value > 0:
                eng.wait_ge(semaphore, value)

        def place(rnd, slot, offset):
            if (offset - slot) % SLOTS:
                return None
            chunk = rnd - (offset - slot) // SLOTS
            return chunk if not isinstance(chunk, int) or 0 <= chunk < CHUNKS else None

        def rounds(eng, one_round):
            for rnd in range(DEPTH + 1):
                one_round(rnd)
            with eng.Fori(DEPTH + 1, CHUNKS) as rnd:
                one_round(rnd)
            for rnd in range(CHUNKS, CHUNKS + DEPTH + 1):
                one_round(rnd)

        def columns(chunk, step=0, steps=STEPS):
            return bass.ds(chunk * C + step * N, steps * N)

        def window(ring, f):
            a = keys[:, ring, f, 0:C]
            return bass.AP(tensor=a.tensor, offset=a.offset, ap=[a.ap[0], [N, 3], [1, C]])

        def over_steps(a):
            return a.unsqueeze(1).broadcast_to([P, STEPS, N])

        def by_step(a):
            return a.rearrange("p (s n) -> p s n", n=N)

        block = ctx.enter_context(nc.Block())

        @block.sync
        def _(sp):
            def load_x(i):
                a, b = X_LOADS[i]
                sp.dma_start(X[:, :, a * C:b * C], x_in[:, :, a * C:b * C]).then_inc(ld_x[i], 16)

            load_x(0)
            sp.dma_start(rnn_w[0][:], rnn0_in).then_inc(ld_first, 16)
            sp.dma_start(h[0][:, 1], cond_in).then_inc(ld_first, 16)
            sp.dma_start(bias[:], bias_in).then_inc(ld_first, 16)
            load_x(1)
            sp.dma_start(h[1][:, 1], cond_in).then_inc(ld_relay, 16)
            sp.dma_start(stage_k, wk_in).then_inc(ld_k, 16)
            sp.dma_start(stage_v, wv_in).then_inc(ld_v, 16)
            sp.dma_start(stage_q, wq_in).then_inc(ld_q, 16)
            load_x(2)
            sp.dma_start(stage_o, wo_in).then_inc(ld_o, 16)
            sp.dma_start(ones[:], ones_in).then_inc(ld_ones, 16)
            load_x(3)
            sp.dma_start(h2[:, 1], cond_in).then_inc(ld_lstm, 16)
            sp.dma_start(lstm_wx[:], lstm_x_in).then_inc(ld_lstm, 16)
            sp.dma_start(lstm_wh[:], lstm_h_in).then_inc(ld_lstm, 16)
            sp.dma_start(rnn_w[1][:], rnn3_in).then_inc(ld_rnn3, 16)
            with sp.Fori(0, CHUNKS) as c:
                sp.wait_ge(x4_done, STEPS * c + STEPS)
                sp.dma_start(out[:, :, columns(c)], X[:, :, columns(c)]).then_inc(stored, 16)
            sp.wait_ge(stored, 16 * CHUNKS)

        @block.gpsimd
        def _(pool):
            def add_scores(c, f):
                if f == 0:
                    return
                wait(pool, prod_done, F * c + f + 1)
                if f == 1:
                    wait(pool, s_mm, c)
                    first = prod[:, 0]
                else:
                    wait(pool, score_add, ADDS * c + f - 1)
                    first = score[:]
                nc.gpsimd.tensor_tensor(score[:], first, prod[:, f % 2], ALU.add).then_inc(score_add, 1)

            def add_mix(c, f):
                wait(pool, mix_done, F * c + f + 1)
                nc.gpsimd.tensor_tensor(mix[:, 0:2], mix[:, 0:2], mix[:, 2:4], ALU.add).then_inc(mix_pair, 1)
                wait(pool, att_lo_done, F * c + f - 1)
                wait(pool, mix_pair, F * c + f + 1)
                nc.gpsimd.tensor_tensor(att[:, f % 2], mix[:, 0], mix[:, 1], ALU.add).then_inc(att_done, 1)

            def one_round(rnd):
                for slot in range(SLOTS):
                    for f in range(F):
                        c = place(rnd, slot, SCORES + f)
                        if c is not None:
                            add_scores(c, f)
                    for f in range(F):
                        c = place(rnd, slot, MIX + f)
                        if c is not None:
                            add_mix(c, f)

            rounds(pool, one_round)

        @block.scalar
        def _(act):
            def split_weights(stage, parts, loaded):
                act.wait_ge(loaded, 16)
                nc.scalar.activation(parts[0][:], stage, ACT.Copy).then_inc(w_hi, 1)

            def split_x1(c):
                wait(act, x1_done, STEPS * c + STEPS)
                wait(act, q_mm, F * (c - XRING + 1))
                nc.scalar.activation(x1_hi[:, c % XRING], X[:, :, columns(c)], ACT.Copy).then_inc(x1_hi_done, 1)

            def keep_keys(c, f):
                if f == 0 and isinstance(c, int) and c == 1:
                    act.wait_ge(w_lo, 2)
                    act.wait_ge(relay_mm, 1)
                wait(act, k_mm, F * c + f + 1)
                wait(act, mix_done, F * (c - KRING + 1) + f + 1)
                b = bias[:, B_K + f:B_K + f + 1]
                nxt = not isinstance(c, int) or c + 1 < CHUNKS
                prv = not isinstance(c, int) or c > 0
                if nxt:
                    nc.scalar.activation(keys[:, (c + 1) % KRING, f, 0:N], ps_k[:, C - N:C], ACT.Identity, bias=b)
                if prv:
                    nc.scalar.activation(keys[:, (c + KRING - 1) % KRING, f, WIN - N:WIN], ps_k[:, 0:N],
                                         ACT.Identity, bias=b)
                nc.scalar.activation(keys[:, c % KRING, f, N:WIN - N], ps_k[:, 0:C],
                                     ACT.Identity, bias=b).then_inc(k_done, 1)

            def rnn_step(layer, c, s):
                wait(act, rnn_mm[layer], STEPS * c + s + 1)
                wait(act, (x1_done, x4_done)[layer], STEPS * c + s - 1)
                b0 = (B_RNN0, B_RNN3)[layer]
                for m in range(KT):
                    last = nc.scalar.activation(h[layer][:, s % 2, m], ps_rnn[layer][:, m * N:(m + 1) * N],
                                                ACT.Tanh, bias=bias[:, b0 + m:b0 + m + 1])
                last.then_inc(rnn_h[layer], 1)

            def lstm_gates(c, s):
                if s == 0 and isinstance(c, int) and c == 0:
                    act.wait_ge(half_done, 1)
                wait(act, lstm_mm, STEPS * c + s + 1)
                wait(act, h2_done, STEPS * c + s)
                for m in range(F):
                    a = ps_lstm[:, m * N:(m + 1) * N]
                    if m < 6:
                        last = nc.scalar.activation(gates[:, m], a, ACT.Tanh, bias=half_bias[:, m:m + 1], scale=0.5)
                    else:
                        last = nc.scalar.activation(gates[:, m], a, ACT.Tanh,
                                                    bias=bias[:, B_LSTM + m:B_LSTM + m + 1])
                last.then_inc(gates_done, 1)

            def lstm_tanh_c(c, s):
                wait(act, cell_chain, 4 * (STEPS * c + s + 1))
                nc.scalar.activation(gates[:, 6:8], cell[:], ACT.Tanh).then_inc(tanh_c, 1)

            def copy_scores(c):
                wait(act, s_mm, c + 1)
                wait(act, softmax, SM * c)
                nc.scalar.activation(W[:].rearrange("p j c -> p (j c)"), ps_s[:], ACT.Copy).then_inc(s_copied, 1)

            def exponentials(c):
                wait(act, softmax, SM * c + 3)
                nc.scalar.activation(W[:], W[:], ACT.Exp, scale=float(HEAD_DIM) ** -0.5).then_inc(exp_done, 1)

            def split_att(c, f):
                wait(act, att_done, F * c + f + 1)
                wait(act, o_mm, F * c + f - 1)
                nc.scalar.activation(att_hi[:, f % 2], att[:, f % 2], ACT.Copy).then_inc(att_hi_done, 1)

            def one_round(rnd):
                if isinstance(rnd, int) and rnd == 1:
                    split_weights(stage_k, wk, ld_k)
                    split_weights(stage_q, wq, ld_q)
                if isinstance(rnd, int) and rnd == 2:
                    split_weights(stage_o, wo, ld_o)
                for slot in range(SLOTS):
                    c = place(rnd, slot, SPLIT)
                    if c is not None:
                        split_x1(c)
                    for s in range(STEPS):
                        c = place(rnd, slot, HIDDEN + 2 * s)
                        if c is not None:
                            lstm_tanh_c(c, s)
                    for s in range(STEPS):
                        c = place(rnd, slot, RNN0 + 2 * s)
                        if c is not None:
                            rnn_step(0, c, s)
                        c = place(rnd, slot, RNN3 + 2 * s)
                        if c is not None:
                            rnn_step(1, c, s)
                    for f in range(F):
                        c = place(rnd, slot, KEYS + f)
                        if c is not None:
                            keep_keys(c, f)
                    for s in range(STEPS):
                        c = place(rnd, slot, LSTM + 2 * s)
                        if c is not None:
                            lstm_gates(c, s)
                    c = place(rnd, slot, HEADSUM)
                    if c is not None:
                        copy_scores(c)
                    c = place(rnd, slot, EXP)
                    if c is not None:
                        exponentials(c)
                    for f in range(F):
                        c = place(rnd, slot, ATTSPLIT + f)
                        if c is not None:
                            split_att(c, f)

            rounds(act, one_round)

        @block.vector
        def _(dve):
            def split_weights(stage, parts, n):
                dve.wait_ge(w_hi, n)
                nc.vector.tensor_tensor(parts[1][:], stage, parts[0][:].bitcast(f32), ALU.subtract).then_inc(w_lo, 1)

            def relay():
                dve.wait_ge(relay_mm, 1)
                for dst, b, half in ((relay_k, B_K, 0), (relay_v, B_V, 1)):
                    last = nc.vector.tensor_tensor(
                        dst[:], ps_s[:, half * 512:(half + 1) * 512].rearrange("p (f n) -> p f n", n=N),
                        bias[:, b:b + F].unsqueeze(2).broadcast_to([P, F, N]), ALU.add)
                last.then_inc(relay_done, 1)

            def add_hidden(hidden, c, s, done):
                xs = X[:, :, columns(c, s, 1)]
                nc.vector.tensor_tensor(xs, hidden[:, s % 2], xs, ALU.add).then_inc(done, 1)

            def split_x1(c):
                wait(dve, x1_done, STEPS * c + STEPS)
                wait(dve, x1_hi_done, c + 1)
                wait(dve, q_mm, F * (c - XRING + 1))
                nc.vector.tensor_tensor(x1_lo[:, c % XRING], X[:, :, columns(c)],
                                        x1_hi[:, c % XRING].bitcast(f32), ALU.subtract).then_inc(x1_lo_done, 1)

            def products(c, f):
                if isinstance(c, int) and c == 0 and f == 0:
                    dve.wait_ge(padded, 1)
                    dve.wait_ge(relay_done, 1)
                    dve.wait_ge(w_lo, 3)
                if isinstance(c, int) and c == CHUNKS - 1 and f == 0:
                    dve.wait_ge(padded, 2)
                wait(dve, q_mm, F * c + f + 1)
                if isinstance(c, int):
                    wait(dve, k_done, F * min(c + 1, CHUNKS - 1) + f + 1)
                else:
                    wait(dve, k_done, F * (c + 1) + f + 1)
                wait(dve, score_add, ADDS * c + (f - 1 if f < 2 else max(f - 2, 1)))
                b = bias[:, B_Q + f:B_Q + f + 1]
                q = ps_q[:, 0:C]
                nc.vector.scalar_tensor_tensor(out=prod[:, f % 2, 0:3], in0=q.unsqueeze(1).broadcast_to([P, 3, C]),
                                               scalar=b, in1=window(c % KRING, f), op0=ALU.add, op1=ALU.mult)
                nc.vector.scalar_tensor_tensor(out=by_step(prod[:, f % 2, 3]), in0=by_step(q), scalar=b,
                                               in1=over_steps(relay_k[:, f]),
                                               op0=ALU.add, op1=ALU.mult).then_inc(prod_done, 1)

            def shift_scores(c):
                wait(dve, s_copied, c + 1)
                nc.vector.tensor_tensor(pair[:], W[:, 0:2], W[:, 2:4], ALU.max).then_inc(softmax, 1)
                wait(dve, softmax, SM * c + 1)
                nc.vector.tensor_tensor(single[:], pair[:, 0], pair[:, 1], ALU.max).then_inc(softmax, 1)
                wait(dve, softmax, SM * c + 2)
                nc.vector.tensor_tensor(W[:], W[:], single[:].unsqueeze(1).broadcast_to([P, J, C]),
                                        ALU.subtract).then_inc(softmax, 1)

            def normalise(c):
                wait(dve, exp_done, c + 1)
                nc.vector.tensor_tensor(pair[:], W[:, 0:2], W[:, 2:4], ALU.add).then_inc(softmax, 1)
                wait(dve, softmax, SM * c + 4)
                nc.vector.tensor_tensor(single[:], pair[:, 0], pair[:, 1], ALU.add).then_inc(softmax, 1)
                wait(dve, softmax, SM * c + 5)
                nc.vector.reciprocal(pair[:, 0], single[:]).then_inc(softmax, 1)
                wait(dve, softmax, SM * c + 6)
                wait(dve, mix_done, F * c)
                nc.vector.tensor_tensor(alpha[:], W[:], pair[:, 0:1].broadcast_to([P, J, C]),
                                        ALU.mult).then_inc(softmax, 1)

            def weigh(c, f):
                wait(dve, softmax, SM * c + SM)
                wait(dve, att_done, F * c + f)
                nc.vector.tensor_tensor(mix[:, 0:3], alpha[:, 0:3], window(c % KRING, f), ALU.mult)
                nc.vector.tensor_tensor(by_step(mix[:, 3]), by_step(alpha[:, 3]), over_steps(relay_v[:, f]),
                                        ALU.mult).then_inc(mix_done, 1)

            def split_att(c, f):
                wait(dve, att_hi_done, F * c + f + 1)
                wait(dve, o_mm, F * c + f - 1)
                nc.vector.tensor_tensor(att_lo[:, f % 2], att[:, f % 2], att_hi[:, f % 2].bitcast(f32),
                                        ALU.subtract).then_inc(att_lo_done, 1)

            def add_attention(c):
                wait(dve, o_mm, F * c + F)
                for m in range(KT):
                    xs = X[:, m, columns(c)]
                    last = nc.vector.scalar_tensor_tensor(out=xs, in0=ps_o[:, m * C:(m + 1) * C],
                                                          scalar=bias[:, B_O + m:B_O + m + 1], in1=xs,
                                                          op0=ALU.add, op1=ALU.add)
                last.then_inc(x2_done, 1)

            def lstm_cell(c, s):
                n = 4 * (STEPS * c + s)
                wait(dve, gates_done, STEPS * c + s + 1)
                nc.vector.tensor_scalar(gates[:, 0:6], gates[:, 0:6], 0.5, 0.5, ALU.mult, ALU.add).then_inc(cell_chain, 1)
                wait(dve, cell_chain, n + 1)
                nc.vector.tensor_tensor(gates[:, 0:2], gates[:, 0:2], gates[:, 6:8], ALU.mult).then_inc(cell_chain, 1)
                nc.vector.tensor_tensor(cell[:], gates[:, 2:4], cell[:], ALU.mult).then_inc(cell_chain, 1)
                wait(dve, cell_chain, n + 3)
                nc.vector.tensor_tensor(cell[:], gates[:, 0:2], cell[:], ALU.add).then_inc(cell_chain, 1)

            def lstm_hidden(c, s):
                wait(dve, tanh_c, STEPS * c + s + 1)
                wait(dve, x3_done, STEPS * c + s - 1)
                nc.vector.tensor_tensor(h2[:, s % 2], gates[:, 4:6], gates[:, 6:8], ALU.mult).then_inc(h2_done, 1)
                wait(dve, h2_done, STEPS * c + s + 1)
                add_hidden(h2, c, s, x3_done)

            nc.vector.memset(cell[:], 0.0)
            nc.vector.memset(keys[:, 0, :, 0:N], 0.0).then_inc(padded, 1)
            dve.wait_ge(padded, 1)

            def one_round(rnd):
                if isinstance(rnd, int) and rnd == 1:
                    split_weights(stage_k, wk, 1)
                    relay()
                    split_weights(stage_q, wq, 2)
                    nc.vector.tensor_scalar(half_bias[:], bias[:, B_LSTM:B_LSTM + 6], 0.5, None,
                                            ALU.mult).then_inc(half_done, 1)
                if isinstance(rnd, int) and rnd == 2:
                    split_weights(stage_o, wo, 3)
                for slot in range(SLOTS):
                    for s in range(STEPS):
                        c = place(rnd, slot, HIDDEN + 2 * s)
                        if c is not None:
                            lstm_hidden(c, s)
                    c = place(rnd, slot, SPLIT)
                    if c is not None:
                        split_x1(c)
                    c = place(rnd, slot, X2)
                    if c is not None:
                        add_attention(c)
                    c = place(rnd, slot, PAD)
                    if isinstance(c, int) and c == CHUNKS - 1:
                        wait(dve, mix_done, F * (c - KRING + 1))
                        nc.vector.memset(keys[:, c % KRING, :, WIN - N:WIN], 0.0).then_inc(padded, 1)
                    for f in range(F):
                        c = place(rnd, slot, SCORES + f)
                        if c is not None:
                            products(c, f)
                    for f in range(F):
                        c = place(rnd, slot, MIX + f)
                        if c is not None:
                            weigh(c, f)
                    c = place(rnd, slot, SHIFT)
                    if c is not None:
                        shift_scores(c)
                    c = place(rnd, slot, NORM)
                    if c is not None:
                        normalise(c)
                    for s in range(STEPS):
                        c = place(rnd, slot, LSTM + 2 * s)
                        if c is not None:
                            lstm_cell(c, s)
                    for s in range(STEPS):
                        c = place(rnd, slot, RNN0 + 2 * s)
                        if c is not None:
                            wait(dve, rnn_h[0], STEPS * c + s + 1)
                            add_hidden(h[0], c, s, x1_done)
                        c = place(rnd, slot, RNN3 + 2 * s)
                        if c is not None:
                            wait(dve, rnn_h[1], STEPS * c + s + 1)
                            add_hidden(h[1], c, s, x4_done)
                    for f in range(F):
                        c = place(rnd, slot, ATTSPLIT + f)
                        if c is not None:
                            split_att(c, f)

            rounds(dve, one_round)

        @block.tensor
        def _(pe):
            def exact_product(dst, weights, moving, start, stop):
                (w_hi_part, w_lo_part), (m_hi, m_lo) = weights, moving
                nc.tensor.matmul(dst, w_hi_part, m_hi, start=start, stop=False, skip_group_check=True)
                nc.tensor.matmul(dst, w_hi_part, m_lo, start=False, stop=False, skip_group_check=True)
                return nc.tensor.matmul(dst, w_lo_part, m_hi, start=False, stop=stop, skip_group_check=True)

            def rnn_step(layer, c, s):
                if isinstance(c, int) and layer == 0 and s == 0:
                    for i, (a, _) in enumerate(X_LOADS):
                        if a == c:
                            pe.wait_ge(ld_x[i], 16)
                if isinstance(c, int) and layer == 0 and s == 0 and c == 0:
                    pe.wait_ge(ld_first, 48)
                if layer == 1:
                    if isinstance(c, int) and c == 0 and s == 0:
                        pe.wait_ge(ld_rnn3, 16)
                    wait(pe, x3_done, STEPS * c + s + 1)
                w = rnn_w[layer]
                wait(pe, rnn_h[layer], STEPS * c + s)
                for m in range(KT):
                    dst = ps_rnn[layer][:, m * N:(m + 1) * N]
                    for k in range(KT):
                        nc.tensor.matmul(dst, w[:, 0, k, m * P:(m + 1) * P], X[:, k, columns(c, s, 1)],
                                         start=(m == 0 and k == 0), stop=False, skip_group_check=True)
                    for k in range(KT):
                        last = nc.tensor.matmul(dst, w[:, 1, k, m * P:(m + 1) * P], h[layer][:, (s + 1) % 2, k],
                                                start=False, stop=(k == KT - 1), skip_group_check=True)
                last.then_inc(rnn_mm[layer], 1)

            def lstm_step(c, s):
                if isinstance(c, int) and c == 0 and s == 0:
                    pe.wait_ge(ld_lstm, 48)
                if s == 0:
                    wait(pe, x2_done, c + 1)
                wait(pe, gates_done, STEPS * c + s)
                for m in range(F):
                    for k in range(KT):
                        nc.tensor.matmul(ps_lstm[:, m * N:(m + 1) * N], lstm_wx[:, k, m * P:(m + 1) * P],
                                         X[:, k, columns(c, s, 1)],
                                         start=(m == 0 and k == 0), stop=False, skip_group_check=True)
                wait(pe, h2_done, STEPS * c + s)
                for m in range(F):
                    for k in range(KT):
                        last = nc.tensor.matmul(ps_lstm[:, m * N:(m + 1) * N], lstm_wh[:, k, m * P:(m + 1) * P],
                                                h2[:, (s + 1) % 2, k],
                                                start=False, stop=(k == KT - 1), skip_group_check=True)
                last.then_inc(lstm_mm, 1)

            def project(dst, w, c, f):
                for k in range(KT):
                    last = exact_product(dst, (w[0][:, k, f], w[1][:, k, f]),
                                         (x1_hi[:, c % XRING, k], x1_lo[:, c % XRING, k]),
                                         start=(k == 0), stop=(k == KT - 1))
                return last

            def project_keys(c, f):
                if isinstance(c, int) and c == 0 and f == 0:
                    pe.wait_ge(w_lo, 1)
                if f == 0:
                    wait(pe, x1_lo_done, c + 1)
                wait(pe, k_done, F * c + f)
                project(ps_k[:, 0:C], wk, c, f).then_inc(k_mm, 1)

            def project_queries(c, f):
                if isinstance(c, int) and c == 0 and f == 0:
                    pe.wait_ge(w_lo, 2)
                wait(pe, prod_done, F * c + f)
                project(ps_q[:, 0:C], wq, c, f).then_inc(q_mm, 1)

            def project_out(c, f):
                if isinstance(c, int) and c == 0 and f == 0:
                    pe.wait_ge(w_lo, 3)
                if f == 0:
                    wait(pe, x2_done, c)
                wait(pe, att_lo_done, F * c + f + 1)
                for m in range(KT):
                    cols = slice(m * P, (m + 1) * P)
                    last = exact_product(ps_o[:, m * C:(m + 1) * C], (wo[0][:, f, cols], wo[1][:, f, cols]),
                                         (att_hi[:, f % 2], att_lo[:, f % 2]),
                                         start=(f == 0 and m == 0), stop=(f == F - 1))
                last.then_inc(o_mm, 1)

            def sum_heads(c):
                if isinstance(c, int) and c == 0:
                    pe.wait_ge(ld_ones, 16)
                    pe.wait_ge(relay_done, 1)
                wait(pe, score_add, ADDS * c + ADDS)
                wait(pe, s_copied, c)
                for half in range(2):
                    last = nc.tensor.matmul(ps_s[:, half * 512:(half + 1) * 512], ones[:],
                                            score[:, 2 * half:2 * half + 2], start=True, stop=True)
                last.then_inc(s_mm, 1)

            def relay():
                pe.wait_ge(ld_k, 16)
                pe.wait_ge(ld_v, 16)
                pe.wait_ge(ld_relay, 16)
                for half, stage in enumerate((stage_k, stage_v)):
                    for f in range(F):
                        for k in range(KT):
                            last = nc.tensor.matmul(ps_s[:, half * 512 + f * N:half * 512 + (f + 1) * N],
                                                    stage[:, k, f], h[1][:, 1, k],
                                                    start=(f == 0 and k == 0), stop=(k == KT - 1),
                                                    skip_group_check=True)
                last.then_inc(relay_mm, 1)

            def one_round(rnd):
                if isinstance(rnd, int) and rnd == 1:
                    relay()
                for slot in range(SLOTS):
                    for s in range(STEPS):
                        c = place(rnd, slot, LSTM + 2 * s)
                        if c is not None:
                            lstm_step(c, s)
                    for s in range(STEPS):
                        c = place(rnd, slot, RNN0 + 2 * s)
                        if c is not None:
                            rnn_step(0, c, s)
                        c = place(rnd, slot, RNN3 + 2 * s)
                        if c is not None:
                            rnn_step(1, c, s)
                    for f in range(F):
                        c = place(rnd, slot, SCORES + f)
                        if c is not None:
                            project_queries(c, f)
                    for f in range(F):
                        c = place(rnd, slot, KEYS + f)
                        if c is not None:
                            project_keys(c, f)
                    for f in range(F):
                        c = place(rnd, slot, OUTPROJ + f)
                        if c is not None:
                            project_out(c, f)
                    c = place(rnd, slot, HEADSUM)
                    if c is not None:
                        sum_heads(c)

            rounds(pe, one_round)


def kernel(x, cond_1024, L0_cond_Wx, L0_cond_Wh, L0_cond_b, L1_cond_WQ_w, L1_cond_WQ_b, L1_cond_WK_w,
           L1_cond_WK_b, L1_cond_WV_w, L1_cond_WV_b, L1_cond_WO_w, L1_cond_WO_b, L2_cond_Wx, L2_cond_Wh,
           L2_cond_b, L3_cond_Wx, L3_cond_Wh, L3_cond_b):
    import concourse.bacc as bacc
    import numpy as np
    from concourse.bass_utils import run_bass_kernel_spmd

    def rows(w):
        w = np.asarray(w)
        return w.reshape(-1, P, w.shape[1]).transpose(1, 0, 2)

    def heads_permuted(w):
        w = np.asarray(w)
        return w.reshape(-1, HEADS, F, PER_TILE).transpose(0, 2, 1, 3).reshape(-1, E)

    def projection(w):
        return rows(heads_permuted(w)).reshape(P, KT, F, P)

    def bias_columns(b):
        return np.asarray(b).reshape(-1, P).T

    def head_bias(b):
        return bias_columns(heads_permuted(np.asarray(b)[None]))

    head_of = np.arange(P) // PER_TILE
    arrays = {
        "x_in": np.asarray(x).transpose(2, 1, 0).reshape(KT, P, T * N).transpose(1, 0, 2),
        "cond_in": np.asarray(cond_1024).T.reshape(KT, P, N).transpose(1, 0, 2),
        "bias_in": np.concatenate([bias_columns(L0_cond_b), bias_columns(L2_cond_b), bias_columns(L3_cond_b),
                                   head_bias(L1_cond_WQ_b), head_bias(L1_cond_WK_b), head_bias(L1_cond_WV_b),
                                   bias_columns(L1_cond_WO_b)], axis=1),
        "ones_in": (head_of[:, None] == head_of[None, :]).astype(np.float32),
        "rnn0_in": np.stack([rows(L0_cond_Wx), rows(L0_cond_Wh)], axis=1),
        "rnn3_in": np.stack([rows(L3_cond_Wx), rows(L3_cond_Wh)], axis=1),
        "lstm_x_in": rows(L2_cond_Wx),
        "lstm_h_in": rows(L2_cond_Wh),
        "wq_in": projection(L1_cond_WQ_w),
        "wk_in": projection(L1_cond_WK_w),
        "wv_in": projection(L1_cond_WV_w),
        "wo_in": rows(heads_permuted(np.asarray(L1_cond_WO_w).T).T),
    }
    arrays = {name: np.ascontiguousarray(a) for name, a in arrays.items()}
    nc = bacc.Bacc("TRN2", target_bir_lowering=False, num_devices=1)
    args = [nc.dram_tensor(name, a.shape, mybir.dt.from_np(a.dtype), kind="ExternalInput").ap()
            for name, a in arrays.items()]
    out = nc.dram_tensor("out", (P, KT, T * N), mybir.dt.float32, kind="ExternalOutput").ap()
    sequence_stack_kernel(nc, *args, out)
    got = np.asarray(run_bass_kernel_spmd(nc, [arrays], core_ids=[0]).results[0]["out"])
    return got.transpose(1, 0, 2).reshape(D, T, N).transpose(2, 1, 0)
```

```python
from contextlib import ExitStack

import concourse.bass as bass
from concourse import mybir

N, T, D = 64, 64, 256
HEADS, HEAD_DIM = 16, 64
E = HEADS * HEAD_DIM
P = 128
KT = D // P
F = E // P
PER_TILE = HEAD_DIM // F
STEPS = 4
C = STEPS * N
CHUNKS = T // STEPS
SLOTS = 8
J = 4
WIN = (STEPS + 2) * N
KRING, XRING = 4, 3

RNN0_X = 0
RNN0 = 1
SPLIT = 8
KEYS = 9
PAD = 17
SCORES = 18
HEADSUM = 27
SHIFT = 27
EXP = 28
NORM = 29
MIX = 30
ATTSPLIT = 31
OUTPROJ = 32
X2 = 39
LSTM_X = 41
LSTM = 42
HIDDEN = 43
RNN3_X = 48
RNN3 = 49
LAST = RNN3 + 2 * (STEPS - 1)
DEPTH = LAST // SLOTS
SM = 7
ADDS = F - 1

B_RNN0, B_LSTM, B_RNN3, B_Q, B_K, B_V, B_O, B_END = 0, 2, 10, 12, 20, 28, 36, 38


def sequence_stack_kernel(nc, x_in, cond_in, bias_in, ones_in, rnn0_in, rnn3_in, lstm_x_in, lstm_h_in,
                          wq_in, wk_in, wv_in, wo_in, out):
    f32, f32r = mybir.dt.float32, mybir.dt.float32r
    ALU, ACT = mybir.AluOpType, mybir.ActivationFunctionType

    ctx = ExitStack()
    with ctx:
        def sb(name, shape, dt=f32):
            return ctx.enter_context(nc.sbuf_tensor(name, [P, *shape], dt))

        def bank(name, banks=1):
            return ctx.enter_context(nc.psum_tensor(name, [P, banks * 512], f32))

        def sem(name):
            return ctx.enter_context(nc.semaphore(name))

        X = sb("X", [KT, T * N])
        rnn_w = [sb("rnn0_w", [2, KT, D]), sb("rnn3_w", [2, KT, D])]
        lstm_wx = sb("lstm_wx", [KT, 4 * D])
        lstm_wh = sb("lstm_wh", [KT, 4 * D])
        wq = [sb("wq_hi", [KT, F, P], f32r), sb("wq_lo", [KT, F, P], f32r)]
        wk = [sb("wk_hi", [KT, F, P], f32r), sb("wk_lo", [KT, F, P], f32r)]
        wo = [sb("wo_hi", [F, D], f32r), sb("wo_lo", [F, D], f32r)]
        bias = sb("bias", [B_END])
        half_bias = sb("half_bias", [F])
        ones = sb("head_ones", [P])
        keys = sb("keys", [KRING, F, WIN])
        relay_k = sb("relay_k", [F, N])
        relay_v = sb("relay_v", [F, N])
        x1_hi = sb("x1_hi", [XRING, KT, C], f32r)
        x1_lo = sb("x1_lo", [XRING, KT, C], f32r)
        prod = sb("prod", [2, J, C])
        score = sb("score", [J, C])
        W = sb("W", [J, C])
        pair = sb("pair", [2, C])
        single = sb("single", [C])
        alpha = sb("alpha", [J, C])
        mix = sb("mix", [J, C])
        att = sb("att", [2, C])
        att_hi = sb("att_hi", [2, C], f32r)
        att_lo = sb("att_lo", [2, C], f32r)
        h = [sb("h0", [2, KT, N]), sb("h3", [2, KT, N])]
        h2 = sb("h2", [2, KT, N])
        gates = sb("gates", [F, N])
        tanh_cell = sb("tanh_cell", [KT, N])
        cell = sb("cell", [KT, N])

        room = keys[:, 2:4].rearrange("p a f w -> p (a f w)")
        stage_k = room[:, 0:KT * E].rearrange("p (k f m) -> p k f m", k=KT, f=F)
        stage_v = room[:, KT * E:2 * KT * E].rearrange("p (k f m) -> p k f m", k=KT, f=F)
        stage_q = room[:, 2 * KT * E:3 * KT * E].rearrange("p (k f m) -> p k f m", k=KT, f=F)
        stage_o = prod[:].rearrange("p a j c -> p (a j c)").rearrange("p (f m) -> p f m", f=F)

        ps_rnn = bank("ps_rnn")
        ps_lstm = bank("ps_lstm", 2)
        ps_q = bank("ps_q")
        ps_k = bank("ps_k")
        ps_s = bank("ps_s", 2)
        ps_o = bank("ps_o")

        ld_first = sem("ld_first")
        ld_x = [sem(f"ld_x{i}") for i in range(4)]
        ld_k, ld_v, ld_q, ld_o = sem("ld_k"), sem("ld_v"), sem("ld_q"), sem("ld_o")
        ld_ones, ld_lstm, ld_rnn3 = sem("ld_ones"), sem("ld_lstm"), sem("ld_rnn3")
        ld_relay = sem("ld_relay")
        X_LOADS = [(0, 1), (1, 2), (2, 6), (6, CHUNKS)]
        w_hi = sem("w_hi")
        w_lo = sem("w_lo")
        relay_mm = sem("relay_mm")
        relay_done = sem("relay_done")
        padded = sem("padded")
        half_done = sem("half_done")
        rnn_mm = sem("rnn_mm")
        lstm_mm = sem("lstm_mm")
        k_mm, q_mm, o_mm = sem("k_mm"), sem("q_mm"), sem("o_mm")
        s_mm = sem("s_mm")
        rnn_h = sem("rnn_h")
        if_done, g_done, o_done = sem("if_done"), sem("g_done"), sem("o_done")
        tanh_c = sem("tanh_c")
        k_done = sem("k_done")
        s_copied, exp_done = sem("s_copied"), sem("exp_done")
        x1_hi_done, att_hi_done = sem("x1_hi_done"), sem("att_hi_done")
        x1_done, x3_done, x4_done = sem("x1_done"), sem("x3_done"), sem("x4_done")
        x1_lo_done, x2_done = sem("x1_lo_done"), sem("x2_done")
        prod_done, mix_done, att_lo_done = sem("prod_done"), sem("mix_done"), sem("att_lo_done")
        softmax = sem("softmax")
        cell_chain = sem("cell_chain")
        o_sigmoid = sem("o_sigmoid")
        h2_done = sem("h2_done")
        score_add = sem("score_add")
        mix_pair = sem("mix_pair")
        att_done = sem("att_done")
        stored = sem("stored")

        def wait(eng, semaphore, value):
            if not isinstance(value, int) or value > 0:
                eng.wait_ge(semaphore, value)

        def place(rnd, slot, offset):
            if (offset - slot) % SLOTS:
                return None
            chunk = rnd - (offset - slot) // SLOTS
            return chunk if not isinstance(chunk, int) or 0 <= chunk < CHUNKS else None

        def rounds(eng, one_round):
            for rnd in range(DEPTH + 1):
                one_round(rnd)
            with nc.Fori(DEPTH + 1, CHUNKS, engines=[eng.engine], hint_back_edge=True) as rnd:
                one_round(rnd)
            for rnd in range(CHUNKS, CHUNKS + DEPTH + 1):
                one_round(rnd)

        def rnn_chunks(rnd, slot, later, offsets=(RNN0, RNN3)):
            chunks = [(layer, place(rnd, slot, offset + later)) for layer, offset in enumerate(offsets)]
            return [(layer, c) for layer, c in chunks if c is not None]

        def rnn_part(layer, m, step, steps):
            at = ((layer * KT + m) * 2 + step) * N
            return ps_rnn[:, at:at + steps * N]

        def lstm_part(m, step, steps):
            at = (m * 2 + step) * N
            return ps_lstm[:, at:at + steps * N]

        def columns(chunk, step=0, steps=STEPS):
            return bass.ds(chunk * C + step * N, steps * N)

        def window(ring, f):
            a = keys[:, ring, f, 0:C]
            return bass.AP(tensor=a.tensor, offset=a.offset, ap=[a.ap[0], [N, 3], [1, C]])

        def over_steps(a):
            return a.unsqueeze(1).broadcast_to([P, STEPS, N])

        def by_step(a):
            return a.rearrange("p (s n) -> p s n", n=N)

        block = ctx.enter_context(nc.Block())

        @block.sync
        def _(sp):
            def load_x(i):
                a, b = X_LOADS[i]
                sp.dma_start(X[:, :, a * C:b * C], x_in[:, :, a * C:b * C]).then_inc(ld_x[i], 16)

            load_x(0)
            sp.dma_start(rnn_w[0][:], rnn0_in).then_inc(ld_first, 16)
            sp.dma_start(h[0][:, 1], cond_in).then_inc(ld_first, 16)
            sp.dma_start(bias[:], bias_in).then_inc(ld_first, 16)
            sp.dma_start(h[1][:, 1], cond_in).then_inc(ld_relay, 16)
            sp.dma_start(stage_k, wk_in).then_inc(ld_k, 16)
            load_x(1)
            sp.dma_start(stage_v, wv_in).then_inc(ld_v, 16)
            sp.dma_start(stage_q, wq_in).then_inc(ld_q, 16)
            load_x(2)
            sp.dma_start(stage_o, wo_in).then_inc(ld_o, 16)
            sp.dma_start(ones[:], ones_in).then_inc(ld_ones, 16)
            load_x(3)
            sp.dma_start(h2[:, 1], cond_in).then_inc(ld_lstm, 16)
            sp.dma_start(lstm_wx[:], lstm_x_in).then_inc(ld_lstm, 16)
            sp.dma_start(lstm_wh[:], lstm_h_in).then_inc(ld_lstm, 16)
            sp.dma_start(rnn_w[1][:], rnn3_in).then_inc(ld_rnn3, 16)
            with sp.Fori(0, CHUNKS) as c:
                sp.wait_ge(x4_done, STEPS * c + STEPS)
                sp.dma_start(out[:, :, columns(c)], X[:, :, columns(c)]).then_inc(stored, 16)
            sp.wait_ge(stored, 16 * CHUNKS)

        @block.gpsimd
        def _(pool):
            def add_scores(c, f):
                if f == 0:
                    return
                wait(pool, prod_done, F * c + f + 1)
                if f == 1:
                    wait(pool, s_mm, c)
                    first = prod[:, 0]
                else:
                    wait(pool, score_add, ADDS * c + f - 1)
                    first = score[:]
                nc.gpsimd.tensor_tensor(score[:], first, prod[:, f % 2], ALU.add).then_inc(score_add, 1)

            def add_mix(c, f):
                wait(pool, mix_done, F * c + f + 1)
                nc.gpsimd.tensor_tensor(mix[:, 0:2], mix[:, 0:2], mix[:, 2:4], ALU.add).then_inc(mix_pair, 1)
                wait(pool, att_lo_done, F * c + f - 1)
                wait(pool, mix_pair, F * c + f + 1)
                nc.gpsimd.tensor_tensor(att[:, f % 2], mix[:, 0], mix[:, 1], ALU.add).then_inc(att_done, 1)

            def one_round(rnd):
                for slot in range(SLOTS):
                    for f in range(F):
                        c = place(rnd, slot, MIX + f)
                        if c is not None:
                            add_mix(c, f)
                    for f in range(F):
                        c = place(rnd, slot, SCORES + f)
                        if c is not None:
                            add_scores(c, f)

            rounds(pool, one_round)

        @block.scalar
        def _(act):
            def split_weights(stage, parts, loaded):
                act.wait_ge(loaded, 16)
                nc.scalar.activation(parts[0][:], stage, ACT.Copy).then_inc(w_hi, 1)

            def split_x1(c):
                wait(act, x1_done, STEPS * c + STEPS)
                wait(act, q_mm, F * (c - XRING + 1))
                nc.scalar.activation(x1_hi[:, c % XRING], X[:, :, columns(c)], ACT.Copy).then_inc(x1_hi_done, 1)

            def keep_keys(c, f):
                if f == 0 and isinstance(c, int) and c == 1:
                    act.wait_ge(w_lo, 2)
                    act.wait_ge(relay_mm, 1)
                wait(act, k_mm, F * c + f + 1)
                wait(act, mix_done, F * (c - KRING + 1) + f + 1)
                b = bias[:, B_K + f:B_K + f + 1]
                nxt = not isinstance(c, int) or c + 1 < CHUNKS
                prv = not isinstance(c, int) or c > 0
                if nxt:
                    nc.scalar.activation(keys[:, (c + 1) % KRING, f, 0:N], ps_k[:, C - N:C], ACT.Identity, bias=b)
                if prv:
                    nc.scalar.activation(keys[:, (c + KRING - 1) % KRING, f, WIN - N:WIN], ps_k[:, 0:N],
                                         ACT.Identity, bias=b)
                nc.scalar.activation(keys[:, c % KRING, f, N:WIN - N], ps_k[:, 0:C],
                                     ACT.Identity, bias=b).then_inc(k_done, 1)

            def rnn_step(rnd, s, chunks):
                wait(act, rnn_mm, STEPS * rnd + s + 1)
                for layer, c in chunks:
                    wait(act, (x1_done, x4_done)[layer], STEPS * c + s - 1)
                    b0 = (B_RNN0, B_RNN3)[layer]
                    for m in range(KT):
                        last = nc.scalar.activation(h[layer][:, s % 2, m], rnn_part(layer, m, s % 2, 1),
                                                    ACT.Tanh, bias=bias[:, b0 + m:b0 + m + 1])
                last.then_inc(rnn_h, 1)

            def lstm_gates(c, s):
                if s == 0 and isinstance(c, int) and c == 0:
                    act.wait_ge(half_done, 1)
                wait(act, h2_done, STEPS * c + s)

                def gate(m, scale, b):
                    return nc.scalar.activation(gates[:, m], lstm_part(m, s % 2, 1), ACT.Tanh, bias=b, scale=scale)

                wait(act, lstm_mm, 2 * (STEPS * c + s) + 1)
                for m in range(4):
                    last = gate(m, 0.5, half_bias[:, m:m + 1])
                last.then_inc(if_done, 1)
                wait(act, lstm_mm, 2 * (STEPS * c + s) + 2)
                for m in (4, 5):
                    last = gate(m, 1.0, bias[:, B_LSTM + m:B_LSTM + m + 1])
                last.then_inc(g_done, 1)
                for m in (6, 7):
                    last = gate(m, 0.5, half_bias[:, m:m + 1])
                last.then_inc(o_done, 1)

            def lstm_tanh_c(c, s):
                wait(act, cell_chain, 4 * (STEPS * c + s + 1))
                nc.scalar.activation(tanh_cell[:], cell[:], ACT.Tanh).then_inc(tanh_c, 1)

            def copy_scores(c):
                wait(act, s_mm, c + 1)
                wait(act, softmax, SM * c)
                nc.scalar.activation(W[:].rearrange("p j c -> p (j c)"), ps_s[:], ACT.Copy).then_inc(s_copied, 1)

            def exponentials(c):
                wait(act, softmax, SM * c + 3)
                nc.scalar.activation(W[:], W[:], ACT.Exp, scale=float(HEAD_DIM) ** -0.5).then_inc(exp_done, 1)

            def split_att(c, f):
                wait(act, att_done, F * c + f + 1)
                wait(act, o_mm, F * c + f - 1)
                nc.scalar.activation(att_hi[:, f % 2], att[:, f % 2], ACT.Copy).then_inc(att_hi_done, 1)

            def one_round(rnd):
                for slot in range(SLOTS):
                    c = place(rnd, slot, SPLIT)
                    if c is not None:
                        split_x1(c)
                    if isinstance(rnd, int) and (rnd, slot) == (1, 0):
                        split_weights(stage_k, wk, ld_k)
                    if isinstance(rnd, int) and (rnd, slot) == (1, 5):
                        split_weights(stage_q, wq, ld_q)
                    if isinstance(rnd, int) and (rnd, slot) == (1, 7):
                        split_weights(stage_o, wo, ld_o)
                    for s in range(STEPS):
                        c = place(rnd, slot, HIDDEN + 2 * s)
                        if c is not None:
                            lstm_tanh_c(c, s)
                    for f in range(F):
                        c = place(rnd, slot, ATTSPLIT + f)
                        if c is not None:
                            split_att(c, f)
                    for s in range(STEPS):
                        chunks = rnn_chunks(rnd, slot, 2 * s)
                        if chunks:
                            rnn_step(rnd, s, chunks)
                    for s in range(STEPS):
                        c = place(rnd, slot, LSTM + 2 * s)
                        if c is not None:
                            lstm_gates(c, s)
                    for f in range(F):
                        c = place(rnd, slot, KEYS + f)
                        if c is not None:
                            keep_keys(c, f)
                    c = place(rnd, slot, EXP)
                    if c is not None:
                        exponentials(c)
                    c = place(rnd, slot, HEADSUM)
                    if c is not None:
                        copy_scores(c)

            rounds(act, one_round)

        @block.vector
        def _(dve):
            def split_weights(stage, parts, n):
                dve.wait_ge(w_hi, n)
                nc.vector.tensor_tensor(parts[1][:], stage, parts[0][:].bitcast(f32), ALU.subtract).then_inc(w_lo, 1)

            def relay():
                dve.wait_ge(relay_mm, 1)
                for dst, b, half in ((relay_k, B_K, 0), (relay_v, B_V, 1)):
                    last = nc.vector.tensor_tensor(
                        dst[:], ps_s[:, half * 512:(half + 1) * 512].rearrange("p (f n) -> p f n", n=N),
                        bias[:, b:b + F].unsqueeze(2).broadcast_to([P, F, N]), ALU.add)
                last.then_inc(relay_done, 1)

            def add_hidden(hidden, c, s, done):
                xs = X[:, :, columns(c, s, 1)]
                nc.vector.tensor_tensor(xs, hidden[:, s % 2], xs, ALU.add).then_inc(done, 1)

            def split_x1(c):
                wait(dve, x1_done, STEPS * c + STEPS)
                wait(dve, x1_hi_done, c + 1)
                wait(dve, q_mm, F * (c - XRING + 1))
                nc.vector.tensor_tensor(x1_lo[:, c % XRING], X[:, :, columns(c)],
                                        x1_hi[:, c % XRING].bitcast(f32), ALU.subtract).then_inc(x1_lo_done, 1)

            def products(c, f):
                if isinstance(c, int) and c == 0 and f == 0:
                    dve.wait_ge(padded, 1)
                    dve.wait_ge(relay_done, 1)
                    dve.wait_ge(w_lo, 3)
                if isinstance(c, int) and c == CHUNKS - 1 and f == 0:
                    dve.wait_ge(padded, 2)
                wait(dve, q_mm, F * c + f + 1)
                if isinstance(c, int):
                    wait(dve, k_done, F * min(c + 1, CHUNKS - 1) + f + 1)
                else:
                    wait(dve, k_done, F * (c + 1) + f + 1)
                wait(dve, score_add, ADDS * c + (f - 1 if f < 2 else max(f - 2, 1)))
                b = bias[:, B_Q + f:B_Q + f + 1]
                q = ps_q[:, 0:C]
                nc.vector.scalar_tensor_tensor(out=prod[:, f % 2, 0:3], in0=q.unsqueeze(1).broadcast_to([P, 3, C]),
                                               scalar=b, in1=window(c % KRING, f), op0=ALU.add, op1=ALU.mult)
                nc.vector.scalar_tensor_tensor(out=by_step(prod[:, f % 2, 3]), in0=by_step(q), scalar=b,
                                               in1=over_steps(relay_k[:, f]),
                                               op0=ALU.add, op1=ALU.mult).then_inc(prod_done, 1)

            def shift_scores(c):
                wait(dve, s_copied, c + 1)
                nc.vector.tensor_tensor(pair[:], W[:, 0:2], W[:, 2:4], ALU.max).then_inc(softmax, 1)
                wait(dve, softmax, SM * c + 1)
                nc.vector.tensor_tensor(single[:], pair[:, 0], pair[:, 1], ALU.max).then_inc(softmax, 1)
                wait(dve, softmax, SM * c + 2)
                nc.vector.tensor_tensor(W[:], W[:], single[:].unsqueeze(1).broadcast_to([P, J, C]),
                                        ALU.subtract).then_inc(softmax, 1)

            def normalise(c):
                wait(dve, exp_done, c + 1)
                nc.vector.tensor_tensor(pair[:], W[:, 0:2], W[:, 2:4], ALU.add).then_inc(softmax, 1)
                wait(dve, softmax, SM * c + 4)
                nc.vector.tensor_tensor(single[:], pair[:, 0], pair[:, 1], ALU.add).then_inc(softmax, 1)
                wait(dve, softmax, SM * c + 5)
                nc.vector.reciprocal(pair[:, 0], single[:]).then_inc(softmax, 1)
                wait(dve, softmax, SM * c + 6)
                wait(dve, mix_done, F * c)
                nc.vector.tensor_tensor(alpha[:], W[:], pair[:, 0:1].broadcast_to([P, J, C]),
                                        ALU.mult).then_inc(softmax, 1)

            def weigh(c, f):
                wait(dve, softmax, SM * c + SM)
                wait(dve, att_done, F * c + f)
                nc.vector.tensor_tensor(mix[:, 0:3], alpha[:, 0:3], window(c % KRING, f), ALU.mult)
                nc.vector.tensor_tensor(by_step(mix[:, 3]), by_step(alpha[:, 3]), over_steps(relay_v[:, f]),
                                        ALU.mult).then_inc(mix_done, 1)

            def split_att(c, f):
                wait(dve, att_hi_done, F * c + f + 1)
                wait(dve, o_mm, F * c + f - 1)
                nc.vector.tensor_tensor(att_lo[:, f % 2], att[:, f % 2], att_hi[:, f % 2].bitcast(f32),
                                        ALU.subtract).then_inc(att_lo_done, 1)

            def add_attention(c):
                wait(dve, o_mm, F * c + F)
                for m in range(KT):
                    xs = X[:, m, columns(c)]
                    last = nc.vector.scalar_tensor_tensor(out=xs, in0=ps_o[:, m * C:(m + 1) * C],
                                                          scalar=bias[:, B_O + m:B_O + m + 1], in1=xs,
                                                          op0=ALU.add, op1=ALU.add)
                last.then_inc(x2_done, 1)

            def lstm_cell(c, s):
                n = 4 * (STEPS * c + s)
                wait(dve, if_done, STEPS * c + s + 1)
                nc.vector.tensor_scalar(gates[:, 0:4], gates[:, 0:4], 0.5, 0.5, ALU.mult, ALU.add).then_inc(cell_chain, 1)
                wait(dve, cell_chain, n + 1)
                nc.vector.tensor_tensor(cell[:], gates[:, 2:4], cell[:], ALU.mult).then_inc(cell_chain, 1)
                wait(dve, g_done, STEPS * c + s + 1)
                nc.vector.tensor_tensor(gates[:, 0:2], gates[:, 0:2], gates[:, 4:6], ALU.mult).then_inc(cell_chain, 1)
                wait(dve, cell_chain, n + 3)
                nc.vector.tensor_tensor(cell[:], gates[:, 0:2], cell[:], ALU.add).then_inc(cell_chain, 1)
                wait(dve, o_done, STEPS * c + s + 1)
                nc.vector.tensor_scalar(gates[:, 6:8], gates[:, 6:8], 0.5, 0.5, ALU.mult, ALU.add).then_inc(o_sigmoid, 1)

            def lstm_hidden(c, s):
                wait(dve, tanh_c, STEPS * c + s + 1)
                wait(dve, o_sigmoid, STEPS * c + s + 1)
                wait(dve, x3_done, STEPS * c + s - 1)
                nc.vector.tensor_tensor(h2[:, s % 2], gates[:, 6:8], tanh_cell[:], ALU.mult).then_inc(h2_done, 1)
                wait(dve, h2_done, STEPS * c + s + 1)
                add_hidden(h2, c, s, x3_done)

            nc.vector.memset(cell[:], 0.0)
            nc.vector.memset(keys[:, 0, :, 0:N], 0.0).then_inc(padded, 1)
            dve.wait_ge(padded, 1)

            def one_round(rnd):
                if isinstance(rnd, int) and rnd == 3:
                    nc.vector.tensor_scalar(half_bias[:], bias[:, B_LSTM:B_LSTM + F], 0.5, None,
                                            ALU.mult).then_inc(half_done, 1)
                for slot in range(SLOTS):
                    for f in range(F):
                        c = place(rnd, slot, SCORES + f)
                        if c is not None:
                            products(c, f)
                    for s in range(STEPS):
                        c = place(rnd, slot, HIDDEN + 2 * s)
                        if c is not None:
                            lstm_hidden(c, s)
                    for f in range(F):
                        c = place(rnd, slot, MIX + f)
                        if c is not None:
                            weigh(c, f)
                    for f in range(F):
                        c = place(rnd, slot, ATTSPLIT + f)
                        if c is not None:
                            split_att(c, f)
                    c = place(rnd, slot, PAD)
                    if isinstance(c, int) and c == CHUNKS - 1:
                        wait(dve, mix_done, F * (c - KRING + 1))
                        nc.vector.memset(keys[:, c % KRING, :, WIN - N:WIN], 0.0).then_inc(padded, 1)
                    c = place(rnd, slot, X2)
                    if c is not None:
                        add_attention(c)
                    for s in range(STEPS):
                        c = place(rnd, slot, LSTM + 2 * s)
                        if c is not None:
                            lstm_cell(c, s)
                    for s in range(STEPS):
                        c = place(rnd, slot, RNN0 + 2 * s)
                        if c is not None:
                            wait(dve, rnn_h, STEPS * rnd + s + 1)
                            add_hidden(h[0], c, s, x1_done)
                        c = place(rnd, slot, RNN3 + 2 * s)
                        if c is not None:
                            wait(dve, rnn_h, STEPS * rnd + s + 1)
                            add_hidden(h[1], c, s, x4_done)
                    c = place(rnd, slot, SPLIT)
                    if c is not None:
                        split_x1(c)
                    if isinstance(rnd, int) and (rnd, slot) == (1, 0):
                        split_weights(stage_k, wk, 1)
                    if isinstance(rnd, int) and (rnd, slot) == (1, 5):
                        split_weights(stage_q, wq, 2)
                    if isinstance(rnd, int) and (rnd, slot) == (1, 7):
                        split_weights(stage_o, wo, 3)
                        relay()
                    c = place(rnd, slot, SHIFT)
                    if c is not None:
                        shift_scores(c)
                    c = place(rnd, slot, NORM)
                    if c is not None:
                        normalise(c)

            rounds(dve, one_round)

        @block.tensor
        def _(pe):
            def exact_product(dst, weights, moving, start, stop):
                (w_hi_part, w_lo_part), (m_hi, m_lo) = weights, moving
                nc.tensor.matmul(dst, w_hi_part, m_hi, start=start, stop=False, skip_group_check=True)
                nc.tensor.matmul(dst, w_hi_part, m_lo, start=False, stop=False, skip_group_check=True)
                return nc.tensor.matmul(dst, w_lo_part, m_hi, start=False, stop=stop, skip_group_check=True)

            def rnn_inputs(rnd, s, chunks):
                wait(pe, rnn_h, STEPS * rnd + s)
                first = True
                for layer, c in chunks:
                    if isinstance(c, int) and layer == 0 and s == 0:
                        for i, (a, _) in enumerate(X_LOADS):
                            if a == c:
                                pe.wait_ge(ld_x[i], 16)
                        if c == 0:
                            pe.wait_ge(ld_first, 48)
                    if layer == 1:
                        if isinstance(c, int) and c == 0 and s == 0:
                            pe.wait_ge(ld_rnn3, 16)
                        wait(pe, x3_done, STEPS * c + s + 2)
                    for m in range(KT):
                        for k in range(KT):
                            nc.tensor.matmul(rnn_part(layer, m, 0, 2), rnn_w[layer][:, 0, k, m * P:(m + 1) * P],
                                             X[:, k, columns(c, s, 2)],
                                             start=first, stop=False, skip_group_check=True)
                            first = False

            def rnn_step(rnd, s, chunks):
                wait(pe, rnn_h, STEPS * rnd + s)
                for layer, _ in chunks:
                    for m in range(KT):
                        for k in range(KT):
                            last = nc.tensor.matmul(rnn_part(layer, m, s % 2, 1),
                                                    rnn_w[layer][:, 1, k, m * P:(m + 1) * P],
                                                    h[layer][:, (s + 1) % 2, k],
                                                    start=False, stop=(k == KT - 1), skip_group_check=True)
                last.then_inc(rnn_mm, 1)

            def lstm_inputs(c, s):
                if isinstance(c, int) and c == 0 and s == 0:
                    pe.wait_ge(ld_lstm, 48)
                if s == 0:
                    wait(pe, x2_done, c + 1)
                for m in range(F):
                    if m == 0:
                        wait(pe, if_done, STEPS * c + s)
                    if m == F // 2:
                        wait(pe, o_done, STEPS * c + s)
                    for k in range(KT):
                        nc.tensor.matmul(lstm_part(m, 0, 2), lstm_wx[:, k, m * P:(m + 1) * P],
                                         X[:, k, columns(c, s, 2)],
                                         start=(m % (F // 2) == 0 and k == 0), stop=False, skip_group_check=True)

            def lstm_step(c, s):
                wait(pe, h2_done, STEPS * c + s)
                for m in range(F):
                    for k in range(KT):
                        last = nc.tensor.matmul(lstm_part(m, s % 2, 1), lstm_wh[:, k, m * P:(m + 1) * P],
                                                h2[:, (s + 1) % 2, k],
                                                start=False, stop=(k == KT - 1), skip_group_check=True)
                    if m % (F // 2) == F // 2 - 1:
                        last.then_inc(lstm_mm, 1)

            def project(dst, w, c, f):
                for k in range(KT):
                    last = exact_product(dst, (w[0][:, k, f], w[1][:, k, f]),
                                         (x1_hi[:, c % XRING, k], x1_lo[:, c % XRING, k]),
                                         start=(k == 0), stop=(k == KT - 1))
                return last

            def project_keys(c, f):
                if isinstance(c, int) and c == 0 and f == 0:
                    pe.wait_ge(w_lo, 1)
                if f == 0:
                    wait(pe, x1_lo_done, c + 1)
                wait(pe, k_done, F * c + f)
                project(ps_k[:, 0:C], wk, c, f).then_inc(k_mm, 1)

            def project_queries(c, f):
                if isinstance(c, int) and c == 0 and f == 0:
                    pe.wait_ge(w_lo, 2)
                wait(pe, prod_done, F * c + f)
                project(ps_q[:, 0:C], wq, c, f).then_inc(q_mm, 1)

            def project_out(c, f):
                if isinstance(c, int) and c == 0 and f == 0:
                    pe.wait_ge(w_lo, 3)
                if f == 0:
                    wait(pe, x2_done, c)
                wait(pe, att_lo_done, F * c + f + 1)
                for m in range(KT):
                    cols = slice(m * P, (m + 1) * P)
                    last = exact_product(ps_o[:, m * C:(m + 1) * C], (wo[0][:, f, cols], wo[1][:, f, cols]),
                                         (att_hi[:, f % 2], att_lo[:, f % 2]),
                                         start=(f == 0 and m == 0), stop=(f == F - 1))
                last.then_inc(o_mm, 1)

            def sum_heads(c):
                if isinstance(c, int) and c == 0:
                    pe.wait_ge(ld_ones, 16)
                    pe.wait_ge(relay_done, 1)
                wait(pe, score_add, ADDS * c + ADDS)
                wait(pe, s_copied, c)
                for half in range(2):
                    last = nc.tensor.matmul(ps_s[:, half * 512:(half + 1) * 512], ones[:],
                                            score[:, 2 * half:2 * half + 2], start=True, stop=True)
                last.then_inc(s_mm, 1)

            def relay():
                pe.wait_ge(ld_k, 16)
                pe.wait_ge(ld_v, 16)
                pe.wait_ge(ld_relay, 16)
                for half, stage in enumerate((stage_k, stage_v)):
                    for f in range(F):
                        for k in range(KT):
                            last = nc.tensor.matmul(ps_s[:, half * 512 + f * N:half * 512 + (f + 1) * N],
                                                    stage[:, k, f], h[1][:, 1, k],
                                                    start=(f == 0 and k == 0), stop=(k == KT - 1),
                                                    skip_group_check=True)
                last.then_inc(relay_mm, 1)

            def one_round(rnd):
                for slot in range(SLOTS):
                    for f in range(F):
                        c = place(rnd, slot, SCORES + f)
                        if c is not None:
                            project_queries(c, f)
                    c = place(rnd, slot, HEADSUM)
                    if c is not None:
                        sum_heads(c)
                    for s in range(STEPS):
                        chunks = rnn_chunks(rnd, slot, 2 * s)
                        if chunks:
                            rnn_step(rnd, s, chunks)
                    for half in range(2):
                        chunks = rnn_chunks(rnd, slot, half * SLOTS // 2, (RNN0_X, RNN3_X))
                        if chunks:
                            rnn_inputs(rnd, 2 * half, chunks)
                        c = place(rnd, slot, LSTM_X + half * SLOTS // 2)
                        if c is not None:
                            lstm_inputs(c, 2 * half)
                    for s in range(STEPS):
                        c = place(rnd, slot, LSTM + 2 * s)
                        if c is not None:
                            lstm_step(c, s)
                    if isinstance(rnd, int) and (rnd, slot) == (1, 6):
                        relay()
                    for f in range(F):
                        c = place(rnd, slot, KEYS + f)
                        if c is not None:
                            project_keys(c, f)
                    for f in range(F):
                        c = place(rnd, slot, OUTPROJ + f)
                        if c is not None:
                            project_out(c, f)

            rounds(pe, one_round)


def kernel(x, cond_1024, L0_cond_Wx, L0_cond_Wh, L0_cond_b, L1_cond_WQ_w, L1_cond_WQ_b, L1_cond_WK_w,
           L1_cond_WK_b, L1_cond_WV_w, L1_cond_WV_b, L1_cond_WO_w, L1_cond_WO_b, L2_cond_Wx, L2_cond_Wh,
           L2_cond_b, L3_cond_Wx, L3_cond_Wh, L3_cond_b):
    import concourse.bacc as bacc
    import numpy as np
    from concourse.bass_utils import run_bass_kernel_spmd

    def rows(w):
        w = np.asarray(w)
        return w.reshape(-1, P, w.shape[1]).transpose(1, 0, 2)

    def heads_permuted(w):
        w = np.asarray(w)
        return w.reshape(-1, HEADS, F, PER_TILE).transpose(0, 2, 1, 3).reshape(-1, E)

    def projection(w):
        return rows(heads_permuted(w)).reshape(P, KT, F, P)

    def bias_columns(b):
        return np.asarray(b).reshape(-1, P).T

    def gates_permuted(w):
        w = np.asarray(w)
        return np.concatenate([w[..., :2 * D], w[..., 3 * D:], w[..., 2 * D:3 * D]], axis=-1)

    def head_bias(b):
        return bias_columns(heads_permuted(np.asarray(b)[None]))

    head_of = np.arange(P) // PER_TILE
    arrays = {
        "x_in": np.asarray(x).transpose(2, 1, 0).reshape(KT, P, T * N).transpose(1, 0, 2),
        "cond_in": np.asarray(cond_1024).T.reshape(KT, P, N).transpose(1, 0, 2),
        "bias_in": np.concatenate([bias_columns(L0_cond_b), bias_columns(gates_permuted(L2_cond_b)), bias_columns(L3_cond_b),
                                   head_bias(L1_cond_WQ_b), head_bias(L1_cond_WK_b), head_bias(L1_cond_WV_b),
                                   bias_columns(L1_cond_WO_b)], axis=1),
        "ones_in": (head_of[:, None] == head_of[None, :]).astype(np.float32),
        "rnn0_in": np.stack([rows(L0_cond_Wx), rows(L0_cond_Wh)], axis=1),
        "rnn3_in": np.stack([rows(L3_cond_Wx), rows(L3_cond_Wh)], axis=1),
        "lstm_x_in": rows(gates_permuted(L2_cond_Wx)),
        "lstm_h_in": rows(gates_permuted(L2_cond_Wh)),
        "wq_in": projection(L1_cond_WQ_w),
        "wk_in": projection(L1_cond_WK_w),
        "wv_in": projection(L1_cond_WV_w),
        "wo_in": rows(heads_permuted(np.asarray(L1_cond_WO_w).T).T),
    }
    arrays = {name: np.ascontiguousarray(a) for name, a in arrays.items()}
    nc = bacc.Bacc("TRN2", target_bir_lowering=False, num_devices=1)
    args = [nc.dram_tensor(name, a.shape, mybir.dt.from_np(a.dtype), kind="ExternalInput").ap()
            for name, a in arrays.items()]
    out = nc.dram_tensor("out", (P, KT, T * N), mybir.dt.float32, kind="ExternalOutput").ap()
    sequence_stack_kernel(nc, *args, out)
    got = np.asarray(run_bass_kernel_spmd(nc, [arrays], core_ids=[0]).results[0]["out"])
    return got.transpose(1, 0, 2).reshape(D, T, N).transpose(2, 1, 0)
```

```python
from contextlib import ExitStack

import concourse.bass as bass
from concourse import mybir

N, T, D = 64, 64, 256
HEADS, HEAD_DIM = 16, 64
E = HEADS * HEAD_DIM
P = 128
KT = D // P
F = E // P
PER_TILE = HEAD_DIM // F
STEPS = 4
C = STEPS * N
CHUNKS = T // STEPS
SLOTS = 8
J = 4
PRODS, MIXES = 4, 2
KRING, XRING = 4, 3

RNN0_X = 0
RNN0 = 1
SPLIT = 8
KEYS = 9
PAD = 17
SCORES = 18
HEADSUM = 27
SHIFT = 27
EXP = 28
NORM = 29
MIX = 30
ATTSPLIT = 31
OUTPROJ = 32
X2 = 39
X2_STEP = 40
LSTM_X = 41
LSTM = 42
HIDDEN = 43
X3 = 45
RNN3_X = 48
RNN3 = 49
WK_SPLIT = 8
WQ_SPLIT = 13
WO_SPLIT = 16
RELAY = 11
RELAY_TILES = 2
RELAY_OUT = 14
LAST = RNN3 + 2 * (STEPS - 1)
DEPTH = LAST // SLOTS
SM = 7
ADDS = F - 1

B_RNN0, B_RNN3, B_Q, B_K, B_O, B_END = 0, 2, 4, 12, 20, 22
G = 4 * P
BIAS_ROWS = (0, 32, 64)


def sequence_stack_kernel(nc, x_in, cond_in, bias_in, v_bias_in, ones_in, rnn0_in, rnn3_in, identity_in,
                          gate_bias_in, bias_rows_in, lstm_x_in, lstm_h_in,
                          wq_in, wk_in, wv_in, wo_in, out):
    f32, f32r, bf16 = mybir.dt.float32, mybir.dt.float32r, mybir.dt.bfloat16
    ALU, ACT = mybir.AluOpType, mybir.ActivationFunctionType

    ctx = ExitStack()
    with ctx:
        def sb(name, shape, dt=f32):
            return ctx.enter_context(nc.sbuf_tensor(name, [P, *shape], dt))

        def bank(name, banks=1):
            return ctx.enter_context(nc.psum_tensor(name, [P, banks * 512], f32))

        def sem(name):
            return ctx.enter_context(nc.semaphore(name))

        X = sb("X", [KT, T * N])
        rnn_w = [sb("rnn0_w", [2, KT, D]), sb("rnn3_w", [2, KT, D])]
        lstm_wx = sb("lstm_wx", [KT, 2, G])
        lstm_wh = sb("lstm_wh", [KT, 2, G])
        wq = [sb("wq_hi", [F, D], f32r), sb("wq_lo", [F, D], f32r)]
        wk = [sb("wk_hi", [F, D], f32r), sb("wk_lo", [F, D], f32r)]
        wo = [sb("wo_hi", [F, D], f32r), sb("wo_lo", [F, D], f32r)]
        bias = sb("bias", [B_END])
        identity = sb("identity", [P])
        gate_bias = sb("gate_bias", [G], bf16)
        bias_rows = sb("bias_rows", [2 * N], bf16)
        ones = sb("head_ones", [P])
        keys = sb("keys", [F, (KRING * STEPS + 2) * N])
        relay_k = sb("relay_k", [F, N])
        relay_v = sb("relay_v", [F, N])
        x1_hi = sb("x1_hi", [XRING, KT, C], f32r)
        x1_lo = sb("x1_lo", [XRING, KT, C], f32r)
        prod = sb("prod", [PRODS, J, C])
        score = sb("score", [J, C])
        W = sb("W", [J, C])
        pair = sb("pair", [2, C])
        single = pair[:, 0]
        alpha = sb("alpha", [J, C])
        mix = sb("mix", [MIXES, J, C])
        att = sb("att", [2, C])
        att_hi = sb("att_hi", [2, C], f32r)
        att_lo = sb("att_lo", [2, C], f32r)
        h = [sb("h0", [2, KT, N]), sb("h3", [2, KT, N])]
        h2 = sb("h2", [KT, N])
        x2_step = sb("x2_step", [KT, N])
        gates = sb("gates", [G])
        gate_i, gate_f, gate_g, gate_o = (gates[:, i * P:(i + 1) * P] for i in range(4))
        cell = sb("cell", [P])
        tanh_cell = gate_g
        new_h = gate_i

        room = keys[:, :, (1 + STEPS) * N:]
        stage_k, stage_v, stage_q = (room[:, :, i * D:(i + 1) * D] for i in range(3))
        gate_bias_stage = mix[:, 0].rearrange("p j c -> p (j c)")[:, 0:G]
        gate_bias_rest = mix[:, 0].rearrange("p j c -> p (j c)")[:, G:2 * G]
        bias_rows_stage = pair[:].rearrange("p a c -> p (a c)")[:, 0:2 * N]
        v_bias = pair[:].rearrange("p a c -> p (a c)")[:, 2 * N:2 * N + F]
        stage_o = prod[:, 0:F * D // (J * C)].rearrange("p a j c -> p (a j c)").rearrange("p (f m) -> p f m", f=F)

        ps_rnn = bank("ps_rnn")
        ps_lstm = bank("ps_lstm", 2)
        ps_q = bank("ps_q")
        ps_k = bank("ps_k")
        ps_s = bank("ps_s", 2)
        ps_o = bank("ps_o")

        ld_first = sem("ld_first")
        ld_x = [sem(f"ld_x{i}") for i in range(4)]
        ld_k, ld_v, ld_q, ld_o = sem("ld_k"), sem("ld_v"), sem("ld_q"), sem("ld_o")
        ld_ones, ld_lstm, ld_rnn3 = sem("ld_ones"), sem("ld_lstm"), sem("ld_rnn3")
        ld_gate_bias = sem("ld_gate_bias")
        ld_relay = sem("ld_relay")
        X_LOADS = [(0, 1), (1, 2), (2, 6), (6, CHUNKS)]
        w_hi = sem("w_hi")
        w_lo = sem("w_lo")
        relay_mm = sem("relay_mm")
        relay_done = sem("relay_done")
        padded = sem("padded")
        bias_split = sem("bias_split")
        rnn_mm = sem("rnn_mm")
        lstm_mm = sem("lstm_mm")
        x_mm = sem("x_mm")
        transposed = sem("transposed")
        k_mm, q_mm, o_mm = sem("k_mm"), sem("q_mm"), sem("o_mm")
        s_mm = sem("s_mm")
        rnn_h = sem("rnn_h")
        if_done, g_done, o_done = sem("if_done"), sem("g_done"), sem("o_done")
        tanh_c = sem("tanh_c")
        x2_kept = sem("x2_kept")
        h2_done = sem("h2_done")
        k_own = sem("k_own")
        k_done = sem("k_done")
        s_copied, exp_done = sem("s_copied"), sem("exp_done")
        x1_hi_done, att_hi_done = sem("x1_hi_done"), sem("att_hi_done")
        x1_done, x3_done, x4_done = sem("x1_done"), sem("x3_done"), sem("x4_done")
        x1_lo_done, x2_done = sem("x1_lo_done"), sem("x2_done")
        prod_done, mix_done, att_lo_done = sem("prod_done"), sem("mix_done"), sem("att_lo_done")
        softmax = sem("softmax")
        cell_chain = sem("cell_chain")
        new_h_done = sem("new_h_done")
        score_add = sem("score_add")
        mix_pair = sem("mix_pair")
        att_done = sem("att_done")
        stored = sem("stored")

        def wait(eng, semaphore, value):
            if not isinstance(value, int) or value > 0:
                eng.wait_ge(semaphore, value)

        def place(rnd, slot, offset):
            if (offset - slot) % SLOTS:
                return None
            chunk = rnd - (offset - slot) // SLOTS
            return chunk if not isinstance(chunk, int) or 0 <= chunk < CHUNKS else None

        def rounds(eng, one_round):
            for rnd in range(DEPTH + 1):
                one_round(rnd)
            with nc.Fori(DEPTH + 1, CHUNKS, engines=[eng.engine], hint_back_edge=True) as rnd:
                one_round(rnd)
            for rnd in range(CHUNKS, CHUNKS + DEPTH + 1):
                one_round(rnd)

        def rnn_chunks(rnd, slot, later, offsets=(RNN0, RNN3)):
            chunks = [(layer, place(rnd, slot, offset + later)) for layer, offset in enumerate(offsets)]
            return [(layer, c) for layer, c in chunks if c is not None]

        def rnn_part(layer, m, step, steps):
            at = ((layer * KT + m) * 2 + step) * N
            return ps_rnn[:, at:at + steps * N]

        def lstm_bank(step, start=0, stop=G):
            return ps_lstm[:, step % 2 * G + start:step % 2 * G + stop]

        def lstm_part(step, half):
            return ps_lstm[half * N:(half + 1) * N, step % 2 * G:(step % 2 + 1) * G]

        def columns(chunk, step=0, steps=STEPS):
            return bass.ds(chunk * C + step * N, steps * N)

        def key_steps(chunk, step, steps=1):
            return bass.ds(chunk % KRING * C + (1 + step) * N, steps * N)

        def window(chunk, f):
            a = keys[:, f, key_steps(chunk, -1, STEPS)]
            return bass.AP(tensor=a.tensor, offset=a.offset, ap=[a.ap[0], [N, 3], [1, C]])

        def transposed_hidden(step):
            return lstm_bank(step, 0, P)

        def over_steps(a):
            return a.unsqueeze(1).broadcast_to([P, STEPS, N])

        def by_step(a):
            return a.rearrange("p (s n) -> p s n", n=N)

        block = ctx.enter_context(nc.Block())

        @block.sync
        def _(sp):
            def load_x(i):
                a, b = X_LOADS[i]
                sp.dma_start(X[:, :, a * C:b * C], x_in[:, :, a * C:b * C]).then_inc(ld_x[i], 16)

            load_x(0)
            sp.dma_start(rnn_w[0][:], rnn0_in).then_inc(ld_first, 16)
            sp.dma_start(h[0][:, 1], cond_in).then_inc(ld_first, 16)
            sp.dma_start(bias[:], bias_in).then_inc(ld_first, 16)
            sp.dma_start(v_bias, v_bias_in).then_inc(ld_v, 16)
            sp.dma_start(h[1][:, 1], cond_in).then_inc(ld_relay, 16)
            sp.dma_start(stage_k, wk_in).then_inc(ld_k, 16)
            load_x(1)
            sp.dma_start(stage_v, wv_in).then_inc(ld_v, 16)
            sp.dma_start(stage_q, wq_in).then_inc(ld_q, 16)
            load_x(2)
            sp.dma_start(stage_o, wo_in).then_inc(ld_o, 16)
            sp.dma_start(ones[:], ones_in).then_inc(ld_ones, 16)
            load_x(3)
            sp.dma_start(gate_bias_stage[0:2], gate_bias_in).then_inc(ld_gate_bias, 16)
            sp.dma_start(bias_rows_stage, bias_rows_in).then_inc(ld_gate_bias, 16)
            sp.dma_start(identity[:], identity_in).then_inc(ld_lstm, 16)
            sp.dma_start(h2[:], cond_in).then_inc(ld_lstm, 16)
            sp.dma_start(lstm_wx[:], lstm_x_in).then_inc(ld_lstm, 16)
            sp.dma_start(lstm_wh[:], lstm_h_in).then_inc(ld_lstm, 16)
            sp.dma_start(rnn_w[1][:], rnn3_in).then_inc(ld_rnn3, 16)
            with sp.Fori(0, CHUNKS) as c:
                sp.wait_ge(x4_done, STEPS * c + STEPS)
                sp.dma_start(out[:, :, columns(c)], X[:, :, columns(c)]).then_inc(stored, 16)
            sp.wait_ge(stored, 16 * CHUNKS)

        @block.gpsimd
        def _(pool):
            def add_scores(c, f):
                if f == 0:
                    return
                wait(pool, prod_done, F * c + f + 1)
                if f == 1:
                    wait(pool, s_mm, c)
                    first = prod[:, 0]
                else:
                    wait(pool, score_add, ADDS * c + f - 1)
                    first = score[:]
                nc.gpsimd.tensor_tensor(score[:], first, prod[:, f % PRODS], ALU.add).then_inc(score_add, 1)

            def add_mix(c, f):
                wait(pool, mix_done, F * c + f + 1)
                m = mix[:, f % MIXES]
                nc.gpsimd.tensor_tensor(m[:, 0:2], m[:, 0:2], m[:, 2:4], ALU.add).then_inc(mix_pair, 1)
                wait(pool, att_lo_done, F * c + f - 1)
                wait(pool, mix_pair, F * c + f + 1)
                nc.gpsimd.tensor_tensor(att[:, f % 2], m[:, 0], m[:, 1], ALU.add).then_inc(att_done, 1)

            def one_round(rnd):
                for slot in range(SLOTS):
                    for f in range(F):
                        c = place(rnd, slot, SCORES + f)
                        if c is not None:
                            add_scores(c, f)
                    for f in range(F):
                        c = place(rnd, slot, MIX + f)
                        if c is not None:
                            add_mix(c, f)
                    for s in range(STEPS):
                        c = place(rnd, slot, RNN3 + 2 * s)
                        if c is not None:
                            wait(pool, rnn_h, STEPS * rnd + s + 1)
                            xs = X[:, :, columns(c, s, 1)]
                            nc.gpsimd.tensor_tensor(xs, h[1][:, s % 2], xs, ALU.add).then_inc(x4_done, 1)

            rounds(pool, one_round)

        @block.scalar
        def _(act):
            def split_weights(stage, parts, loaded):
                act.wait_ge(loaded, 16)
                nc.scalar.activation(parts[0][:], stage, ACT.Copy).then_inc(w_hi, 1)

            def split_x1(c):
                wait(act, x1_done, STEPS * c + STEPS)
                wait(act, q_mm, F * (c - XRING + 1))
                nc.scalar.activation(x1_hi[:, c % XRING], X[:, :, columns(c)], ACT.Copy).then_inc(x1_hi_done, 1)

            def keep_keys(c, f):
                if f == 0 and isinstance(c, int) and c == 1:
                    act.wait_ge(w_lo, 2)
                    act.wait_ge(relay_mm, 1)
                wait(act, k_mm, F * c + f + 1)
                wait(act, mix_done, F * (c - KRING + 1) + f + 1)
                b = bias[:, B_K + f:B_K + f + 1]
                nxt = not isinstance(c, int) or c + 1 < CHUNKS
                prv = not isinstance(c, int) or c > 0
                nc.scalar.activation(keys[:, f, key_steps(c, 0, STEPS)], ps_k[:, 0:C],
                                     ACT.Identity, bias=b).then_inc(k_own, 1)
                wait(act, k_own, F * c + f + 1)
                if prv:
                    last = nc.scalar.activation(keys[:, f, key_steps(c + KRING - 1, STEPS)], ps_k[:, 0:N],
                                                ACT.Identity, bias=b)
                if nxt:
                    last = nc.scalar.activation(keys[:, f, key_steps(c + 1, -1)], ps_k[:, C - N:C],
                                                ACT.Identity, bias=b)
                last.then_inc(k_done, 1)

            def rnn_step(rnd, s, chunks):
                wait(act, rnn_mm, STEPS * rnd + s + 1)
                for layer, c in chunks:
                    wait(act, (x1_done, x4_done)[layer], STEPS * c + s - 1)
                    b0 = (B_RNN0, B_RNN3)[layer]
                    for m in range(KT):
                        last = nc.scalar.activation(h[layer][:, s % 2, m], rnn_part(layer, m, s % 2, 1),
                                                    ACT.Tanh, bias=bias[:, b0 + m:b0 + m + 1])
                last.then_inc(rnn_h, 1)

            def lstm_gates(c, s):
                wait(act, h2_done, STEPS * c + s)
                wait(act, lstm_mm, STEPS * c + s + 1)
                nc.scalar.activation(gates[:, 0:2 * P], lstm_bank(s, 0, 2 * P), ACT.Tanh,
                                     scale=0.5).then_inc(if_done, 1)
                nc.scalar.activation(gate_g, lstm_bank(s, 2 * P, 3 * P), ACT.Tanh).then_inc(g_done, 1)
                nc.scalar.activation(gate_o, lstm_bank(s, 3 * P, G), ACT.Tanh,
                                     scale=0.5).then_inc(o_done, 1)

            def lstm_tanh_c(c, s):
                wait(act, cell_chain, 3 * (STEPS * c + s + 1))
                nc.scalar.activation(tanh_cell, cell[:], ACT.Tanh, scale=0.5).then_inc(tanh_c, 1)

            def keep_x2(c, s):
                if s == 0:
                    wait(act, x2_done, c + 1)
                wait(act, x_mm, STEPS * c + s)
                nc.scalar.activation(x2_step[:], X[:, :, columns(c, s, 1)], ACT.Copy).then_inc(x2_kept, 1)

            def keep_hidden(c, s):
                wait(act, transposed, STEPS * c + s + 1)
                wait(act, x3_done, STEPS * c + s)
                nc.scalar.activation(h2[:].rearrange("p k n -> p (k n)"), transposed_hidden(s),
                                     ACT.Copy, scale=0.5).then_inc(h2_done, 1)

            def copy_scores(c):
                wait(act, s_mm, c + 1)
                wait(act, softmax, SM * c)
                nc.scalar.activation(W[:].rearrange("p j c -> p (j c)"), ps_s[:], ACT.Copy).then_inc(s_copied, 1)

            def exponentials(c):
                wait(act, softmax, SM * c + 3)
                nc.scalar.activation(W[:], W[:], ACT.Exp, scale=float(HEAD_DIM) ** -0.5).then_inc(exp_done, 1)

            def split_att(c, f):
                wait(act, att_done, F * c + f + 1)
                wait(act, o_mm, F * c + f - 1)
                nc.scalar.activation(att_hi[:, f % 2], att[:, f % 2], ACT.Copy).then_inc(att_hi_done, 1)

            def one_round(rnd):
                for slot in range(SLOTS):
                    c = place(rnd, slot, SPLIT)
                    if c is not None:
                        split_x1(c)
                    if isinstance(rnd, int) and rnd * SLOTS + slot == WK_SPLIT:
                        split_weights(stage_k, wk, ld_k)
                    if isinstance(rnd, int) and rnd * SLOTS + slot == WQ_SPLIT:
                        split_weights(stage_q, wq, ld_q)
                    if isinstance(rnd, int) and rnd * SLOTS + slot == WO_SPLIT:
                        split_weights(stage_o, wo, ld_o)
                    for s in range(STEPS):
                        c = place(rnd, slot, HIDDEN + 2 * s)
                        if c is not None:
                            lstm_tanh_c(c, s)
                    for s in range(STEPS):
                        c = place(rnd, slot, X2_STEP + 2 * s)
                        if c is not None:
                            keep_x2(c, s)
                    c = place(rnd, slot, EXP)
                    if c is not None:
                        exponentials(c)
                    c = place(rnd, slot, HEADSUM)
                    if c is not None:
                        copy_scores(c)
                    for s in range(STEPS):
                        c = place(rnd, slot, LSTM + 2 * s)
                        if c is not None:
                            lstm_gates(c, s)
                    for s in range(STEPS):
                        chunks = rnn_chunks(rnd, slot, 2 * s)
                        if chunks:
                            rnn_step(rnd, s, chunks)
                    for f in range(F):
                        c = place(rnd, slot, KEYS + f)
                        if c is not None:
                            keep_keys(c, f)
                    for s in range(STEPS):
                        c = place(rnd, slot, HIDDEN + 2 * s)
                        if c is not None:
                            keep_hidden(c, s)
                    for f in range(F):
                        c = place(rnd, slot, ATTSPLIT + f)
                        if c is not None:
                            split_att(c, f)

            rounds(act, one_round)

        @block.vector
        def _(dve):
            def split_weights(stage, parts, n):
                dve.wait_ge(w_hi, n)
                nc.vector.tensor_tensor(parts[1][:], stage, parts[0][:].bitcast(f32), ALU.subtract).then_inc(w_lo, 1)

            def relay():
                dve.wait_ge(relay_mm, 1)
                for dst, b, half in ((relay_k, bias[:, B_K:B_K + F], 0), (relay_v, v_bias, 1)):
                    last = nc.vector.tensor_tensor(
                        dst[:], ps_s[:, half * 512:(half + 1) * 512].rearrange("p (f n) -> p f n", n=N),
                        b.unsqueeze(2).broadcast_to([P, F, N]), ALU.add)
                last.then_inc(relay_done, 1)

            def split_x1(c):
                wait(dve, x1_done, STEPS * c + STEPS)
                wait(dve, x1_hi_done, c + 1)
                wait(dve, q_mm, F * (c - XRING + 1))
                nc.vector.tensor_tensor(x1_lo[:, c % XRING], X[:, :, columns(c)],
                                        x1_hi[:, c % XRING].bitcast(f32), ALU.subtract).then_inc(x1_lo_done, 1)

            def products(c, f):
                if isinstance(c, int) and c == 0 and f == 0:
                    dve.wait_ge(padded, 1)
                    dve.wait_ge(relay_done, 1)
                    dve.wait_ge(w_lo, 3)
                if isinstance(c, int) and c == CHUNKS - 1 and f == 0:
                    dve.wait_ge(padded, 2)
                wait(dve, q_mm, F * c + f + 1)
                if isinstance(c, int):
                    wait(dve, k_done, F * min(c + 1, CHUNKS - 1) + f + 1)
                else:
                    wait(dve, k_done, F * (c + 1) + f + 1)
                wait(dve, score_add, ADDS * c + (f - PRODS + 1 if f < PRODS else max(f - PRODS, 1)))
                b = bias[:, B_Q + f:B_Q + f + 1]
                q = ps_q[:, 0:C]
                nc.vector.scalar_tensor_tensor(out=prod[:, f % PRODS, 0:3], in0=q.unsqueeze(1).broadcast_to([P, 3, C]),
                                               scalar=b, in1=window(c, f), op0=ALU.add, op1=ALU.mult)
                nc.vector.scalar_tensor_tensor(out=by_step(prod[:, f % PRODS, 3]), in0=by_step(q), scalar=b,
                                               in1=over_steps(relay_k[:, f]),
                                               op0=ALU.add, op1=ALU.mult).then_inc(prod_done, 1)

            def shift_scores(c):
                wait(dve, s_copied, c + 1)
                nc.vector.tensor_tensor(pair[:], W[:, 0:2], W[:, 2:4], ALU.max).then_inc(softmax, 1)
                wait(dve, softmax, SM * c + 1)
                nc.vector.tensor_tensor(single, pair[:, 0], pair[:, 1], ALU.max).then_inc(softmax, 1)
                wait(dve, softmax, SM * c + 2)
                nc.vector.tensor_tensor(W[:], W[:], single.unsqueeze(1).broadcast_to([P, J, C]),
                                        ALU.subtract).then_inc(softmax, 1)

            def normalise(c):
                wait(dve, exp_done, c + 1)
                nc.vector.tensor_tensor(pair[:], W[:, 0:2], W[:, 2:4], ALU.add).then_inc(softmax, 1)
                wait(dve, softmax, SM * c + 4)
                nc.vector.tensor_tensor(single, pair[:, 0], pair[:, 1], ALU.add).then_inc(softmax, 1)
                wait(dve, softmax, SM * c + 5)
                nc.vector.reciprocal(pair[:, 0], single).then_inc(softmax, 1)
                wait(dve, softmax, SM * c + 6)
                wait(dve, mix_done, F * c)
                nc.vector.tensor_tensor(alpha[:], W[:], pair[:, 0:1].broadcast_to([P, J, C]),
                                        ALU.mult).then_inc(softmax, 1)

            def weigh(c, f):
                wait(dve, softmax, SM * c + SM)
                wait(dve, att_done, F * c + f - MIXES + 1)
                nc.vector.tensor_tensor(mix[:, f % MIXES, 0:3], alpha[:, 0:3], window(c, f), ALU.mult)
                nc.vector.tensor_tensor(by_step(mix[:, f % MIXES, 3]), by_step(alpha[:, 3]), over_steps(relay_v[:, f]),
                                        ALU.mult).then_inc(mix_done, 1)

            def split_att(c, f):
                wait(dve, att_hi_done, F * c + f + 1)
                wait(dve, o_mm, F * c + f - 1)
                nc.vector.tensor_tensor(att_lo[:, f % 2], att[:, f % 2], att_hi[:, f % 2].bitcast(f32),
                                        ALU.subtract).then_inc(att_lo_done, 1)

            def add_attention(c):
                wait(dve, o_mm, F * c + F)
                for m in range(KT):
                    xs = X[:, m, columns(c)]
                    last = nc.vector.scalar_tensor_tensor(out=xs, in0=ps_o[:, m * C:(m + 1) * C],
                                                          scalar=bias[:, B_O + m:B_O + m + 1], in1=xs,
                                                          op0=ALU.add, op1=ALU.add)
                last.then_inc(x2_done, 1)

            def lstm_cell(c, s):
                n = 3 * (STEPS * c + s)
                wait(dve, if_done, STEPS * c + s + 1)
                nc.vector.scalar_tensor_tensor(out=gate_f, in0=gate_f, scalar=1.0, in1=cell[:],
                                               op0=ALU.add, op1=ALU.mult).then_inc(cell_chain, 1)
                wait(dve, g_done, STEPS * c + s + 1)
                nc.vector.scalar_tensor_tensor(out=gate_i, in0=gate_i, scalar=1.0, in1=gate_g,
                                               op0=ALU.add, op1=ALU.mult).then_inc(cell_chain, 1)
                wait(dve, cell_chain, n + 2)
                nc.vector.scalar_tensor_tensor(out=cell[:], in0=gate_f, scalar=0.5, in1=gate_i,
                                               op0=ALU.mult, op1=ALU.add).then_inc(cell_chain, 1)

            def lstm_hidden(c, s):
                wait(dve, o_done, STEPS * c + s + 1)
                wait(dve, tanh_c, STEPS * c + s + 1)
                nc.vector.scalar_tensor_tensor(out=new_h, in0=gate_o, scalar=1.0, in1=tanh_cell,
                                               op0=ALU.add, op1=ALU.mult).then_inc(new_h_done, 1)

            def split_gate_bias():
                def step(instruction):
                    instruction.then_inc(bias_split, 1)

                first_row, mid_row, hi_row = BIAS_ROWS
                rest, part = gate_bias_rest[0:2], gate_bias[first_row:first_row + 2]
                dve.wait_ge(ld_gate_bias, 32)
                dve.wait_ge(bias_split, 1)
                nc.vector.tensor_copy(bias_rows[:], bias_rows_stage)
                step(nc.vector.tensor_copy(part, gate_bias_stage[0:2]))
                dve.wait_ge(bias_split, 2)
                nc.vector.tensor_copy(gate_bias[hi_row:hi_row + 2], part)
                step(nc.vector.tensor_tensor(rest, gate_bias_stage[0:2], part, ALU.subtract))
                dve.wait_ge(bias_split, 3)
                step(nc.vector.tensor_copy(part, rest))
                dve.wait_ge(bias_split, 4)
                nc.vector.tensor_copy(gate_bias[mid_row:mid_row + 2], part)
                step(nc.vector.tensor_tensor(rest, rest, part, ALU.subtract))
                dve.wait_ge(bias_split, 5)
                step(nc.vector.tensor_copy(part, rest))

            nc.vector.memset(cell[:], 0.0)
            nc.vector.memset(gate_bias[:], 0.0).then_inc(bias_split, 1)
            nc.vector.memset(keys[:, :, 0:N], 0.0).then_inc(padded, 1)
            dve.wait_ge(padded, 1)

            def one_round(rnd):
                if isinstance(rnd, int) and rnd == 2:
                    split_gate_bias()
                for slot in range(SLOTS):
                    c = place(rnd, slot, PAD)
                    if isinstance(c, int) and c == CHUNKS - 1:
                        wait(dve, mix_done, F * (c - KRING + 1))
                        nc.vector.memset(keys[:, :, key_steps(c, STEPS)], 0.0).then_inc(padded, 1)
                    for s in range(STEPS):
                        c = place(rnd, slot, HIDDEN + 2 * s)
                        if c is not None:
                            lstm_hidden(c, s)
                        c = place(rnd, slot, X3 + 2 * s)
                        if c is not None:
                            wait(dve, h2_done, STEPS * c + s + 1)
                            xs = X[:, :, columns(c, s, 1)]
                            nc.vector.tensor_tensor(xs, h2[:], xs, ALU.add).then_inc(x3_done, 1)
                    for f in range(F):
                        c = place(rnd, slot, SCORES + f)
                        if c is not None:
                            products(c, f)
                    for f in range(F):
                        c = place(rnd, slot, MIX + f)
                        if c is not None:
                            weigh(c, f)
                    c = place(rnd, slot, SPLIT)
                    if c is not None:
                        split_x1(c)
                    if isinstance(rnd, int) and rnd * SLOTS + slot == WK_SPLIT:
                        split_weights(stage_k, wk, 1)
                    if isinstance(rnd, int) and rnd * SLOTS + slot == WQ_SPLIT:
                        split_weights(stage_q, wq, 2)
                    if isinstance(rnd, int) and rnd * SLOTS + slot == WO_SPLIT:
                        split_weights(stage_o, wo, 3)
                    if isinstance(rnd, int) and rnd * SLOTS + slot == RELAY_OUT:
                        relay()
                    c = place(rnd, slot, NORM)
                    if c is not None:
                        normalise(c)
                    c = place(rnd, slot, X2)
                    if c is not None:
                        add_attention(c)
                    for s in range(STEPS):
                        c = place(rnd, slot, LSTM + 2 * s)
                        if c is not None:
                            lstm_cell(c, s)
                    c = place(rnd, slot, SHIFT)
                    if c is not None:
                        shift_scores(c)
                    for s in range(STEPS):
                        c = place(rnd, slot, RNN0 + 2 * s)
                        if c is not None:
                            wait(dve, rnn_h, STEPS * rnd + s + 1)
                            xs = X[:, :, columns(c, s, 1)]
                            nc.vector.tensor_tensor(xs, h[0][:, s % 2], xs, ALU.add).then_inc(x1_done, 1)
                    for f in range(F):
                        c = place(rnd, slot, ATTSPLIT + f)
                        if c is not None:
                            split_att(c, f)

            rounds(dve, one_round)

        @block.tensor
        def _(pe):
            def exact_product(dst, weights, moving, start, stop):
                (w_hi_part, w_lo_part), (m_hi, m_lo) = weights, moving
                nc.tensor.matmul(dst, w_hi_part, m_hi, start=start, stop=False, skip_group_check=True)
                nc.tensor.matmul(dst, w_hi_part, m_lo, start=False, stop=False, skip_group_check=True)
                return nc.tensor.matmul(dst, w_lo_part, m_hi, start=False, stop=stop, skip_group_check=True)

            def rnn_inputs(rnd, s, chunks):
                wait(pe, rnn_h, STEPS * rnd + s)
                first = True
                for layer, c in chunks:
                    if isinstance(c, int) and layer == 0 and s == 0:
                        for i, (a, _) in enumerate(X_LOADS):
                            if a == c:
                                pe.wait_ge(ld_x[i], 16)
                        if c == 0:
                            pe.wait_ge(ld_first, 48)
                    if layer == 1:
                        if isinstance(c, int) and c == 0 and s == 0:
                            pe.wait_ge(ld_rnn3, 16)
                        wait(pe, x3_done, STEPS * c + s + 2)
                    for m in range(KT):
                        for k in range(KT):
                            nc.tensor.matmul(rnn_part(layer, m, 0, 2), rnn_w[layer][:, 0, k, m * P:(m + 1) * P],
                                             X[:, k, columns(c, s, 2)],
                                             start=first, stop=False, skip_group_check=True)
                            first = False

            def rnn_step(rnd, s, chunks):
                wait(pe, rnn_h, STEPS * rnd + s)
                for layer, _ in chunks:
                    for m in range(KT):
                        for k in range(KT):
                            last = nc.tensor.matmul(rnn_part(layer, m, s % 2, 1),
                                                    rnn_w[layer][:, 1, k, m * P:(m + 1) * P],
                                                    h[layer][:, (s + 1) % 2, k],
                                                    start=False, stop=(k == KT - 1), skip_group_check=True)
                last.then_inc(rnn_mm, 1)

            def lstm_inputs(c, s):
                if isinstance(c, int) and c == 0 and s == 0:
                    pe.wait_ge(ld_lstm, 64)
                    pe.wait_ge(bias_split, 6)
                wait(pe, x2_kept, STEPS * c + s + 1)
                wait(pe, h2_done, STEPS * c + s - 1)
                nc.tensor.matmul(lstm_bank(s), bias_rows[:], gate_bias[:],
                                 start=True, stop=False, skip_group_check=True)
                for k in range(KT):
                    for half in range(2):
                        last = nc.tensor.matmul(lstm_part(s, half), x2_step[:, k], lstm_wx[:, k, half],
                                                start=False, stop=False, skip_group_check=True)
                last.then_inc(x_mm, 1)

            def lstm_step(c, s):
                wait(pe, h2_done, STEPS * c + s)
                for k in range(KT):
                    for half in range(2):
                        last = nc.tensor.matmul(lstm_part(s, half), h2[:, k], lstm_wh[:, k, half],
                                                start=False, stop=(k == KT - 1), skip_group_check=True)
                last.then_inc(lstm_mm, 1)

            def transpose_hidden(c, s):
                wait(pe, new_h_done, STEPS * c + s + 1)
                nc.tensor.matmul(transposed_hidden(s), new_h, identity[:], start=True, stop=True,
                                 is_transpose=True, skip_group_check=True).then_inc(transposed, 1)

            def project(dst, w, c, f):
                for k in range(KT):
                    rows = slice(k * P, (k + 1) * P)
                    last = exact_product(dst, (w[0][:, f, rows], w[1][:, f, rows]),
                                         (x1_hi[:, c % XRING, k], x1_lo[:, c % XRING, k]),
                                         start=(k == 0), stop=(k == KT - 1))
                return last

            def project_keys(c, f):
                if isinstance(c, int) and c == 0 and f == 0:
                    pe.wait_ge(w_lo, 1)
                if f == 0:
                    wait(pe, x1_lo_done, c + 1)
                wait(pe, k_done, F * c + f)
                project(ps_k[:, 0:C], wk, c, f).then_inc(k_mm, 1)

            def project_queries(c, f):
                if isinstance(c, int) and c == 0 and f == 0:
                    pe.wait_ge(w_lo, 2)
                wait(pe, prod_done, F * c + f)
                project(ps_q[:, 0:C], wq, c, f).then_inc(q_mm, 1)

            def project_out(c, f):
                if isinstance(c, int) and c == 0 and f == 0:
                    pe.wait_ge(w_lo, 3)
                if f == 0:
                    wait(pe, x2_done, c)
                wait(pe, att_lo_done, F * c + f + 1)
                for m in range(KT):
                    cols = slice(m * P, (m + 1) * P)
                    last = exact_product(ps_o[:, m * C:(m + 1) * C], (wo[0][:, f, cols], wo[1][:, f, cols]),
                                         (att_hi[:, f % 2], att_lo[:, f % 2]),
                                         start=(f == 0 and m == 0), stop=(f == F - 1))
                last.then_inc(o_mm, 1)

            def sum_heads(c):
                if isinstance(c, int) and c == 0:
                    pe.wait_ge(ld_ones, 16)
                    pe.wait_ge(relay_done, 1)
                wait(pe, score_add, ADDS * c + ADDS)
                wait(pe, s_copied, c)
                for half in range(2):
                    last = nc.tensor.matmul(ps_s[:, half * 512:(half + 1) * 512], ones[:],
                                            score[:, 2 * half:2 * half + 2], start=True, stop=True)
                last.then_inc(s_mm, 1)

            def relay(f):
                if f == 0:
                    pe.wait_ge(ld_k, 16)
                    pe.wait_ge(ld_v, 32)
                    pe.wait_ge(ld_relay, 16)
                for half, stage in enumerate((stage_k, stage_v)):
                    for k in range(KT):
                        last = nc.tensor.matmul(ps_s[:, half * 512 + f * N:half * 512 + (f + 1) * N],
                                                stage[:, f, k * P:(k + 1) * P], h[1][:, 1, k],
                                                start=(f == 0 and k == 0), stop=(k == KT - 1),
                                                skip_group_check=True)
                if f == F - 1:
                    last.then_inc(relay_mm, 1)

            def one_round(rnd):
                for slot in range(SLOTS):
                    for f in range(F):
                        c = place(rnd, slot, SCORES + f)
                        if c is not None:
                            project_queries(c, f)
                    for s in range(STEPS):
                        c = place(rnd, slot, LSTM + 2 * s)
                        if c is not None:
                            lstm_step(c, s)
                    c = place(rnd, slot, HEADSUM)
                    if c is not None:
                        sum_heads(c)
                    for s in range(STEPS):
                        chunks = rnn_chunks(rnd, slot, 2 * s)
                        if chunks:
                            rnn_step(rnd, s, chunks)
                    for f in range(F):
                        c = place(rnd, slot, KEYS + f)
                        if c is not None:
                            project_keys(c, f)
                    for half in range(2):
                        chunks = rnn_chunks(rnd, slot, half * SLOTS // 2, (RNN0_X, RNN3_X))
                        if chunks:
                            rnn_inputs(rnd, 2 * half, chunks)
                    for s in range(STEPS):
                        c = place(rnd, slot, LSTM_X + 2 * s)
                        if c is not None:
                            lstm_inputs(c, s)
                    for s in range(STEPS):
                        c = place(rnd, slot, HIDDEN + 2 * s)
                        if c is not None:
                            transpose_hidden(c, s)
                    for f in range(F):
                        if isinstance(rnd, int) and rnd * SLOTS + slot == RELAY + f // RELAY_TILES:
                            relay(f)
                    for f in range(F):
                        c = place(rnd, slot, OUTPROJ + f)
                        if c is not None:
                            project_out(c, f)

            rounds(pe, one_round)


def kernel(x, cond_1024, L0_cond_Wx, L0_cond_Wh, L0_cond_b, L1_cond_WQ_w, L1_cond_WQ_b, L1_cond_WK_w,
           L1_cond_WK_b, L1_cond_WV_w, L1_cond_WV_b, L1_cond_WO_w, L1_cond_WO_b, L2_cond_Wx, L2_cond_Wh,
           L2_cond_b, L3_cond_Wx, L3_cond_Wh, L3_cond_b):
    import concourse.bacc as bacc
    import numpy as np
    from concourse.bass_utils import run_bass_kernel_spmd

    def rows(w):
        w = np.asarray(w)
        return w.reshape(-1, P, w.shape[1]).transpose(1, 0, 2)

    def heads_permuted(w):
        w = np.asarray(w)
        return w.reshape(-1, HEADS, F, PER_TILE).transpose(0, 2, 1, 3).reshape(-1, E)

    def projection(w):
        return rows(heads_permuted(w)).reshape(P, KT, F, P).transpose(0, 2, 1, 3).reshape(P, F, D)

    def bias_columns(b):
        return np.asarray(b).reshape(-1, P).T

    def gates_permuted(w):
        w = np.asarray(w).reshape(-1, 4, 2, P)[:, [0, 1, 3, 2]]
        return w.transpose(0, 2, 1, 3).reshape(-1, 4 * D)

    def head_bias(b):
        return bias_columns(heads_permuted(np.asarray(b)[None]))

    head_of = np.arange(P) // PER_TILE
    bias_rows = np.zeros((P, 2, N), np.float32)
    for half in range(2):
        bias_rows[np.array(BIAS_ROWS) + half, half] = 1
    arrays = {
        "x_in": np.asarray(x).transpose(2, 1, 0).reshape(KT, P, T * N).transpose(1, 0, 2),
        "cond_in": np.asarray(cond_1024).T.reshape(KT, P, N).transpose(1, 0, 2),
        "bias_in": np.concatenate([bias_columns(L0_cond_b), bias_columns(L3_cond_b),
                                   head_bias(L1_cond_WQ_b), head_bias(L1_cond_WK_b),
                                   bias_columns(L1_cond_WO_b)], axis=1),
        "v_bias_in": head_bias(L1_cond_WV_b),
        "ones_in": (head_of[:, None] == head_of[None, :]).astype(np.float32),
        "rnn0_in": np.stack([rows(L0_cond_Wx), rows(L0_cond_Wh)], axis=1),
        "rnn3_in": np.stack([rows(L3_cond_Wx), rows(L3_cond_Wh)], axis=1),
        "identity_in": np.eye(P, dtype=np.float32),
        "gate_bias_in": gates_permuted(L2_cond_b).reshape(2, G),
        "bias_rows_in": bias_rows.reshape(P, 2 * N),
        "lstm_x_in": rows(gates_permuted(L2_cond_Wx)).reshape(P, KT, 2, G),
        "lstm_h_in": rows(gates_permuted(L2_cond_Wh)).reshape(P, KT, 2, G),
        "wq_in": projection(L1_cond_WQ_w),
        "wk_in": projection(L1_cond_WK_w),
        "wv_in": projection(L1_cond_WV_w),
        "wo_in": rows(heads_permuted(np.asarray(L1_cond_WO_w).T).T),
    }
    arrays = {name: np.ascontiguousarray(a) for name, a in arrays.items()}
    nc = bacc.Bacc("TRN2", target_bir_lowering=False, num_devices=1)
    args = [nc.dram_tensor(name, a.shape, mybir.dt.from_np(a.dtype), kind="ExternalInput").ap()
            for name, a in arrays.items()]
    out = nc.dram_tensor("out", (P, KT, T * N), mybir.dt.float32, kind="ExternalOutput").ap()
    sequence_stack_kernel(nc, *args, out)
    got = np.asarray(run_bass_kernel_spmd(nc, [arrays], core_ids=[0]).results[0]["out"])
    return got.transpose(1, 0, 2).reshape(D, T, N).transpose(2, 1, 0)
```
